# Optimizing a Trainium2 kernel written in Bass

```python
import numpy as np
import jax
import jax.numpy as jnp

def _softmax(x, axis=-1):
    return jax.nn.softmax(x, axis=axis)

def _gelu(x):
    return jax.nn.gelu(x, approximate=True)

def _silu(x):
    return jax.nn.silu(x)

def _sigmoid(x):
    return jax.nn.sigmoid(x)

def _layernorm(x, axis=-1, eps=1e-05):
    m = jnp.mean(x, axis=axis, keepdims=True)
    v = jnp.var(x, axis=axis, keepdims=True)
    return (x - m) / jnp.sqrt(v + eps)

def _scatter_add(tgt, idx, src, axis=0):
    return tgt.at[idx].add(src)

def _segment_sum(src, seg, n):
    return jax.ops.segment_sum(src, seg, n)
kernel_name = 'mk_flamingo_gated_d1_seqx_r8_81054f'

def setup_inputs(seed: int=0):
    np.random.seed(seed)
    _w = jnp.asarray

    def _rec_inputs():
        import jax
        import jax.numpy as jnp
        _rk = jax.random.key(seed)
        x = 0.01048 + 0.1018 * jax.random.normal(jax.random.fold_in(_rk, 1), (4, 256, 256), jnp.float32)
        _lenS = 256 - jax.random.randint(jax.random.fold_in(_rk, 7), (4,), 0, max(1, 256 // 4) + 1, jnp.int32)
        _lenS2 = 256 - jax.random.randint(jax.random.fold_in(_rk, 8), (4,), 0, max(1, 256 // 4) + 1, jnp.int32)
        _ctx_512P = jax.random.normal(jax.random.fold_in(_rk, 11), (4, 16, 64), jnp.float32)
        _ctx_512c = jax.random.dirichlet(jax.random.fold_in(_rk, 511), 0.3 * jnp.ones((16,), jnp.float32), (4, 256))
        _ctx_512t = jnp.einsum('bsk,bkd->bsd', _ctx_512c, _ctx_512P)
        _ctx_512t = _ctx_512t * jax.lax.rsqrt(jnp.mean(jnp.square(_ctx_512t)) + 1e-12) * 0.953939
        ctx_512 = -0.000292821 + 1.00034 * (_ctx_512t + 0.3 * jax.random.normal(jax.random.fold_in(_rk, 611), (4, 256, 64), jnp.float32))
        _g = jax.random.normal(jax.random.fold_in(_rk, 9001), (2, 1), jnp.float32)
        _g = jnp.sign(_g) * jnp.maximum(jnp.abs(_g), 1.0) + (_g == 0) * 1.0
        g_xattn = _g[0]
        g_ffn = _g[1]
        return (x, ctx_512, g_xattn, g_ffn)
    x, ctx_512, g_xattn, g_ffn = _rec_inputs()

    def _L0_xattn_setup():
        import jax, jax.numpy as jnp
        import numpy as np
        LRELU_ALPHA = 0.2
        MASK_VAL = -10000000000.0
        B, N, F_IN = (4, 256, 64)
        H, F_OUT = (8, 32)
        F_HID = H * F_OUT

        def gat_layer(x, adj, W, a_self, a_neigh, b):
            feat = jnp.einsum('nf,hfo->hno', x, W)
            attn_self = jnp.einsum('hno,ho->hn', feat, a_self)
            attn_neigh = jnp.einsum('hno,ho->hn', feat, a_neigh)
            e = attn_self[:, :, None] + attn_neigh[:, None, :]
            e = jax.nn.leaky_relu(e, LRELU_ALPHA)
            e = e + MASK_VAL * (1.0 - adj)[None, :, :]
            alpha = jax.nn.softmax(e, axis=-1)
            out = jnp.einsum('hnm,hmo->hno', alpha, feat) + b[:, None, :]
            out = jnp.transpose(out, (1, 0, 2)).reshape(out.shape[1], -1)
            return jax.nn.elu(out)
        key = jax.random.key(seed)
        ks = jax.random.split(key, 10)
        feats = jax.random.normal(ks[0], (B, N, F_IN), dtype=jnp.float32)
        a = (jax.random.uniform(ks[1], (B, N, N)) < 0.01).astype(jnp.float32)
        adj = jnp.maximum(a, jnp.eye(N, dtype=jnp.float32)[None])
        s0 = 1.0 / np.sqrt(F_IN)
        s1 = 1.0 / np.sqrt(F_HID)
        return {'feats': feats, 'adj': adj, 'W0': jax.random.normal(ks[2], (H, F_IN, F_OUT), dtype=jnp.float32) * s0, 'a_self0': jax.random.normal(ks[3], (H, F_OUT), dtype=jnp.float32) * 0.1, 'a_neigh0': jax.random.normal(ks[4], (H, F_OUT), dtype=jnp.float32) * 0.1, 'b0': jnp.zeros((H, F_OUT), dtype=jnp.float32), 'W1': jax.random.normal(ks[5], (H, F_HID, F_OUT), dtype=jnp.float32) * s1, 'a_self1': jax.random.normal(ks[6], (H, F_OUT), dtype=jnp.float32) * 0.1, 'a_neigh1': jax.random.normal(ks[7], (H, F_OUT), dtype=jnp.float32) * 0.1, 'b1': jnp.zeros((H, F_OUT), dtype=jnp.float32)}
    _L0_xattn_all = _L0_xattn_setup()
    _L0_xattn_in = {k: v for k, v in _L0_xattn_all.items() if k in ('W0', 'a_self0', 'a_neigh0', 'b0', 'W1', 'a_self1', 'a_neigh1', 'b1')}
    del _L0_xattn_all

    def _L0_ffn_setup():
        import jax, jax.numpy as jnp
        import numpy as np
        D = 256
        H_TOTAL = 1024
        E = 8
        K = 2
        HE = H_TOTAL // E
        B, S = (2, 256)
        key = jax.random.key(seed)
        ks = jax.random.split(key, 8)
        scale_up = 1.0 / np.sqrt(D)
        scale_dn = 1.0 / np.sqrt(HE)
        return {'x': jax.random.normal(ks[0], (B, S, D), dtype=jnp.float32), 'Wg1': jax.random.normal(ks[1], (E, D), dtype=jnp.float32) * 0.02, 'Wg2': jax.random.normal(ks[2], (E, E), dtype=jnp.float32) * 0.2, 'Wup': jax.random.uniform(ks[3], (E, HE, D), dtype=jnp.float32, minval=-scale_up, maxval=scale_up), 'bup': jax.random.uniform(ks[4], (E, HE), dtype=jnp.float32, minval=-scale_up, maxval=scale_up), 'Wdown': jax.random.uniform(ks[5], (E, D, HE), dtype=jnp.float32, minval=-scale_dn, maxval=scale_dn), 'bdown': jax.random.uniform(ks[6], (E, D), dtype=jnp.float32, minval=-scale_dn, maxval=scale_dn)}
    _L0_ffn_all = _L0_ffn_setup()
    _L0_ffn_in = {k: v for k, v in _L0_ffn_all.items() if k in ('Wg1', 'Wg2', 'Wup', 'bup', 'Wdown', 'bdown')}
    del _L0_ffn_all
    return {'x': x, 'ctx_512': ctx_512, 'g_xattn': g_xattn, 'g_ffn': g_ffn, 'L0_xattn_W0': _L0_xattn_in['W0'], 'L0_xattn_a_self0': _L0_xattn_in['a_self0'], 'L0_xattn_a_neigh0': _L0_xattn_in['a_neigh0'], 'L0_xattn_b0': _L0_xattn_in['b0'], 'L0_xattn_W1': _L0_xattn_in['W1'], 'L0_xattn_a_self1': _L0_xattn_in['a_self1'], 'L0_xattn_a_neigh1': _L0_xattn_in['a_neigh1'], 'L0_xattn_b1': _L0_xattn_in['b1'], 'L0_ffn_Wg1': _L0_ffn_in['Wg1'], 'L0_ffn_Wg2': _L0_ffn_in['Wg2'], 'L0_ffn_Wup': _L0_ffn_in['Wup'], 'L0_ffn_bup': _L0_ffn_in['bup'], 'L0_ffn_Wdown': _L0_ffn_in['Wdown'], 'L0_ffn_bdown': _L0_ffn_in['bdown']}

def reference(x, ctx_512, g_xattn, g_ffn, L0_xattn_W0, L0_xattn_a_self0, L0_xattn_a_neigh0, L0_xattn_b0, L0_xattn_W1, L0_xattn_a_self1, L0_xattn_a_neigh1, L0_xattn_b1, L0_ffn_Wg1, L0_ffn_Wg2, L0_ffn_Wup, L0_ffn_bup, L0_ffn_Wdown, L0_ffn_bdown):
    import jax
    import jax.numpy as jnp

    def _L0_xattn_ref(feats, adj, W0, a_self0, a_neigh0, b0, W1, a_self1, a_neigh1, b1):
        import jax, jax.numpy as jnp
        import numpy as np
        LRELU_ALPHA = 0.2
        MASK_VAL = -10000000000.0
        B, N, F_IN = (4, 256, 64)
        H, F_OUT = (8, 32)
        F_HID = H * F_OUT

        def gat_layer(x, adj, W, a_self, a_neigh, b):
            feat = jnp.einsum('nf,hfo->hno', x, W)
            attn_self = jnp.einsum('hno,ho->hn', feat, a_self)
            attn_neigh = jnp.einsum('hno,ho->hn', feat, a_neigh)
            e = attn_self[:, :, None] + attn_neigh[:, None, :]
            e = jax.nn.leaky_relu(e, LRELU_ALPHA)
            e = e + MASK_VAL * (1.0 - adj)[None, :, :]
            alpha = jax.nn.softmax(e, axis=-1)
            out = jnp.einsum('hnm,hmo->hno', alpha, feat) + b[:, None, :]
            out = jnp.transpose(out, (1, 0, 2)).reshape(out.shape[1], -1)
            return jax.nn.elu(out)

        def per_graph(x, a):
            h = gat_layer(x, a, W0, a_self0, a_neigh0, b0)
            return gat_layer(h, a, W1, a_self1, a_neigh1, b1)
        return jax.vmap(per_graph)(feats, adj)

    def _L0_ffn_ref(x, Wg1, Wg2, Wup, bup, Wdown, bdown):
        import jax, jax.numpy as jnp
        import numpy as np
        D = 256
        H_TOTAL = 1024
        E = 8
        K = 2
        HE = H_TOTAL // E
        B, S = (2, 256)
        Bd, Sd, Dd = x.shape
        T = Bd * Sd
        xt = x.reshape(T, Dd)
        logits = jnp.tanh(xt @ Wg1.T) @ Wg2.T
        _, top_idx = jax.lax.top_k(logits, K)
        top_logits = jnp.take_along_axis(logits, top_idx, axis=1)
        top_scores = jax.nn.softmax(top_logits.astype(jnp.float32), axis=1).astype(logits.dtype)
        rows = jnp.arange(T)[:, None]
        scores = jnp.zeros_like(logits).at[rows, top_idx].set(top_scores)
        up = jnp.einsum('td,ehd->teh', xt, Wup) + bup
        h = jax.nn.silu(up)
        down = jnp.einsum('teh,eoh->teo', h, Wdown) + bdown
        out = jnp.einsum('te,teo->to', scores, down)
        return out.reshape(Bd, Sd, Dd)
    x = x + jnp.tanh(g_xattn[0]) * _L0_xattn_ref(ctx_512, _layernorm(x, axis=-1), L0_xattn_W0, L0_xattn_a_self0, L0_xattn_a_neigh0, L0_xattn_b0, L0_xattn_W1, L0_xattn_a_self1, L0_xattn_a_neigh1, L0_xattn_b1)
    x = x + jnp.tanh(g_ffn[0]) * _L0_ffn_ref(_layernorm(x, axis=-1), L0_ffn_Wg1, L0_ffn_Wg2, L0_ffn_Wup, L0_ffn_bup, L0_ffn_Wdown, L0_ffn_bdown)
    return x

_drawn_inputs = setup_inputs


def setup_inputs(seed=0):
    import zlib

    import numpy as np

    out = dict(_drawn_inputs(seed))
    spreads = {'L0_xattn_b0': (0.0, 0.1), 'L0_xattn_b1': (0.0, 0.1)}
    factors = {'L0_ffn_bup': 3.966}
    for name, (base, spread) in spreads.items():
        noise = np.random.default_rng([zlib.crc32(name.encode()), seed]).standard_normal(out[name].shape)
        drawn = base * np.exp(spread * noise) if base else spread * noise
        out[name] = jnp.asarray(drawn.astype(out[name].dtype))
    for name, factor in factors.items():
        out[name] = (out[name] * factor).astype(out[name].dtype)
    return out
```

```python
from contextlib import ExitStack

import numpy as np

import concourse.bass as bass
from concourse import mybir

ALU = mybir.AluOpType
ACT = mybir.ActivationFunctionType
AX = mybir.AxisListType
F32 = mybir.dt.float32
F32R = mybir.dt.float32r
BF16 = mybir.dt.bfloat16
I32 = mybir.dt.int32
U32 = mybir.dt.uint32

P = 128
B, N, D = 4, 256, 256
FIN = 64
H, FO = 8, 32
E, HE = 8, 128
T = B * N
NT = T // P
C = N // P
HALVES = 2
HT = T // HALVES
TH = NT // HALVES
SLOTS = 3
LAG = 2
EPS = 1e-5
MASK = 1e10
LRELU = 0.2


def build(nc, x, ctx_in, ctx_t, g2, w0, w0_t, b0_c, b0_r, w1, w1_t, b1_r, avec, wg1, wg2_r, wup, bup_c, wdown, bdown, out):
    with ExitStack() as stack:
        def sb(name, shape, dt=F32):
            return stack.enter_context(nc.sbuf_tensor(name, shape, dt))

        def sem(name):
            return stack.enter_context(nc.semaphore(name))

        x_sb = sb("x_sb", [P, NT, D])
        ctx_sb = sb("ctx_sb", [P, NT, FIN])
        gates = sb("gates", [P, 2])
        w0_sb = sb("w0_sb", [P, H * FO])
        w0t_sb = sb("w0t_sb", [P, C, FIN])
        b0_sb = sb("b0_sb", [P, C])
        w1_sb = sb("w1_sb", [P, C, H * FO])
        w1t_sb = sb("w1t_sb", [P, C, H * FO])
        b1_sb = sb("b1_sb", [64, H * FO])
        a_sb = sb("a_sb", [H, 4, FO])
        wg1_sb = sb("wg1_sb", [P, C, E])
        wg2_sb = sb("wg2_sb", [P, E, E])
        wup_sb = sb("wup_sb", [P, C, E * HE])
        bup_sb = sb("bup_sb", [P, E])
        wdown_sb = sb("wdown_sb", [P, E, D])
        bdown_sb = sb("bdown_sb", [2 * E, D])
        w0_hi, w0_lo = sb("w0_hi", [P, H * FO], F32R), sb("w0_lo", [P, H * FO], F32R)
        w1_hi, w1_lo = sb("w1_hi", [P, C, H * FO], F32R), sb("w1_lo", [P, C, H * FO], F32R)
        wup_hi, wup_lo = sb("wup_hi", [P, C, E * HE], F32R), sb("wup_lo", [P, C, E * HE], F32R)
        wdown_hi, wdown_lo = sb("wdown_hi", [P, E, D], F32R), sb("wdown_lo", [P, E, D], F32R)
        bdown_hi, bdown_lo = sb("bdown_hi", [2 * E, D], F32R), sb("bdown_lo", [2 * E, D], F32R)
        wg1_parts = sb("wg1_parts", [P, C, 2 * E], F32R)
        b1_hi = sb("b1_hi", [64, H * FO], F32R)
        b1_parts = sb("b1_parts", [64, H * FO], F32R)
        ctx_parts = sb("ctx_parts", [P, NT, 2 * FIN], F32R)
        ident = sb("ident", [P, P])
        ident_bf = sb("ident_bf", [P, P], BF16)
        ones = sb("ones", [P, P])
        ones_r = sb("ones_r", [64, P], F32R)
        pick = sb("pick", [2 * E, E, P], F32R)
        expert_no = sb("expert_no", [P, TH, E])
        half_power = sb("half_power", [P, NT])
        top = sb("top", [P, NT, 8])
        onehot = sb("onehot", [P, NT, N], BF16)
        onehot_t = sb("onehot_t", [P, B, C, N], F32R)
        once = sb("once", [P, B, C, 2 * FIN], F32R)
        twice = sb("twice", [P, T], F32R)
        exp0 = sb("exp0", [P, C, T])
        h1 = sb("h1", [P, C, T])
        h1_hi, h1_lo = sb("h1_hi", [P, C, T], F32R), sb("h1_lo", [P, C, T], F32R)
        exp1 = exp0[:].rearrange("p c (t n) -> p (c t) n", n=D)
        xa = sb("xa", [P, NT, D])
        peaks = sb("peaks", [P, 8])
        peaks_all = sb("peaks_all", [P, 8])
        bound = sb("bound", [P, 8])
        xstat = sb("xstat", [P, NT, 6])
        xmv = sb("xmv", [P, NT, 2])
        xrstd = sb("xrstd", [P, NT])
        lead = sb("lead", [P, NT])
        need = sb("need", [P, NT])
        spare = sb("spare", [P, NT])
        good = sb("good", [P, NT])
        good_all = sb("good_all", [P, NT])
        flag_f = sb("flag_f", [P, 1])
        flag = sb("flag", [P, 1], I32)
        stat = sb("stat", [P, NT, 6])
        mv = sb("mv", [P, NT, 2])
        veps = sb("veps", [P, NT])
        rstd = sb("rstd", [P, NT])
        xn = sb("xn", [P, NT, D])
        xt_hi, xt_lo = sb("xt_hi", [P, C, T], F32R), sb("xt_lo", [P, C, T], F32R)
        gate_in = sb("gate_in", [P, TH, E])
        gate_h = sb("gate_h", [P, TH, E])
        gate_prod = sb("gate_prod", [P, TH, E, E])
        logits = sb("logits", [P, TH, E])
        ltop = sb("ltop", [P, TH, 8])
        lidx = sb("lidx", [P, TH, 8], U32)
        lidx_f = sb("lidx_f", [P, TH, 8])
        ldiff = sb("ldiff", [P, TH])
        lth = sb("lth", [P, TH])
        prob = sb("prob", [P, 2, TH])
        hit = sb("hit", [P, 2, TH, E])
        score_k = sb("score_k", [P, 2, TH, E])
        score = sb("score", [P, TH, E])
        score_hi = sb("score_hi", [P, TH, E], F32R)
        score_parts = sb("score_parts", [P, TH, 2 * E])
        score_t = sb("score_t", [2 * E, T], F32R)
        act_out = sb("act_out", [P, 2, HT])
        hid = sb("hid", [P, 2, HT])
        hid_hi, hid_lo = sb("hid_hi", [P, SLOTS, HT], F32R), sb("hid_lo", [P, SLOTS, HT], F32R)
        out_sb = sb("out_sb", [P, NT, D])
        pick_f = out_sb[0:2 * E, 0:E * P // D, :].rearrange("k a (b n) -> k (a b) n", n=P)
        def slots(t):
            flat = t.rearrange("p a b -> p (a b)")
            return [flat[:, k * C * N:(k + 1) * C * N].rearrange("p (c n) -> p c n", c=C) for k in range(4)]

        gz, gexp, pr, alpha_t = slots(exp0[:])
        sc, sc2, alpha, gh = slots(h1[:])
        feat, fprod, gh_t, spare_slot = slots(out_sb[:])
        mask, a01_bc, a23_bc, b_bc = slots(xn[:])
        gu = fprod
        diag = spare_slot[:, 0, :].rearrange("p (c n) -> p c n", c=C)
        ctxt_b = spare_slot[0:FIN, 1, :]
        a_bc = [a01_bc[:, 0:1, :], a01_bc[:, 1:2, :], a23_bc[:, 0:1, :], a23_bc[:, 1:2, :]]
        gve = sb("gve", [P, C])
        grstd = sb("grstd", [P, C])
        att = sb("att", [P, 2, C, H])
        nmax = sb("nmax", [P, C])
        psum_p = sb("psum_p", [P, C])
        rsum = sb("rsum", [P, C])

        bank = stack.enter_context(nc.psum_tensor("bank", [P, 8, 512], F32))
        UP, PICK, DOWN, XT, ROUTE = (4, 5), 3, (6, 7), (0, 1), 2

        x_in = [sem(f"x_in{b}") for b in range(B)]
        ctx_ld, w0_ld, w1_ld, small_ld, check_ld = (sem(n) for n in ("ctx_ld", "w0_ld", "w1_ld", "small_ld", "check_ld"))
        wup_ld, wdown_ld, gate_ld, bdown_ld, b1_ld = (sem(n) for n in ("wup_ld", "wdown_ld", "gate_ld", "bdown_ld", "b1_ld"))
        const_raw, const_rdy, pick_rdy = sem("const_raw"), sem("const_rdy"), sem("pick_rdy")
        ones_rdy, gates_rdy = sem("ones_rdy"), sem("gates_rdy")
        ctx_hi_rdy, ctx_rdy = sem("ctx_hi_rdy"), sem("ctx_rdy")
        w0_rdy, w1_rdy, wup_rdy, wdown_rdy, small_rdy, b1_rdy, bdown_rdy, wg1_rdy = (
            sem(n) for n in ("w0_rdy", "w1_rdy", "wup_rdy", "wdown_rdy", "small_rdy", "b1_rdy", "bdown_rdy", "wg1_rdy"))
        top_rdy, onehot_rdy, turned, onehot_t_rdy = (sem(n) for n in ("top_rdy", "onehot_rdy", "turned", "onehot_t_rdy"))
        once_mm, once_rdy, twice_mm, twice_rdy = (sem(n) for n in ("once_mm", "once_rdy", "twice_mm", "twice_rdy"))
        feat0_mm, exp0_rdy, elu0_part, h1_rdy, h1_hi_rdy, h1_lo_rdy = (
            sem(n) for n in ("feat0_mm", "exp0_rdy", "elu0_part", "h1_rdy", "h1_hi_rdy", "h1_lo_rdy"))
        feat1_mm, exp1_rdy, elu1_part, elu1_rdy, xa_rdy = (
            sem(n) for n in ("feat1_mm", "exp1_rdy", "elu1_part", "elu1_rdy", "xa_rdy"))
        peaks_part, peaks_rdy, peaks_all_rdy, pool_step, xstat_rdy, flag_step, good_rdy, flag_rdy = (
            sem(n) for n in ("peaks_part", "peaks_rdy", "peaks_all_rdy", "pool_step", "xstat_rdy", "flag_step",
                             "good_rdy", "flag_rdy"))
        stat_rdy, mv_rdy, veps_rdy, rstd_rdy, xn_rdy, xt_mm, xt_hi_rdy, xt_lo_rdy = (
            sem(n) for n in ("stat_rdy", "mv_rdy", "veps_rdy", "rstd_rdy", "xn_rdy", "xt_mm", "xt_hi_rdy", "xt_lo_rdy"))
        gate_mm, gate_in_rdy, gate_h_rdy, route_step, ldiff_rdy, lth_rdy, score_rdy, score_mm, score_t_rdy = (
            sem(n) for n in ("gate_mm", "gate_in_rdy", "gate_h_rdy", "route_step", "ldiff_rdy", "lth_rdy", "score_rdy",
                             "score_mm", "score_t_rdy"))
        up_mm, pick_mm, silu_rdy, hid_rdy, hid_hi_rdy, hid_lo_rdy, down_mm, out_mm, out_rdy, stored = (
            sem(n) for n in ("up_mm", "pick_mm", "silu_rdy", "hid_rdy", "hid_hi_rdy", "hid_lo_rdy", "down_mm", "out_mm",
                             "out_rdy", "stored"))
        g_bc_ld, g_graph_ld, g_vec, g_sqrt, g_feat_mm, g_feat, g_att, g_diag, g_row_mm, g_max, g_exp = (
            sem(n) for n in ("g_bc_ld", "g_graph_ld", "g_vec", "g_sqrt", "g_feat_mm", "g_feat", "g_att", "g_diag",
                             "g_row_mm", "g_max", "g_exp"))
        g_alpha, g_alpha_mm, g_alpha_t, g_out_mm, g_z, g_zexp, g_h, g_h_mm, g_h_t, g_xa = (
            sem(n) for n in ("g_alpha", "g_alpha_mm", "g_alpha_t", "g_out_mm", "g_z", "g_zexp", "g_h", "g_h_mm", "g_h_t",
                             "g_xa"))

        block = stack.enter_context(nc.Block())

        def tok(half):
            return slice(half * HT, (half + 1) * HT)

        def tiles(half):
            return slice(half * TH, (half + 1) * TH)

        def pair(q):
            return slice(2 * q, 2 * q + 2)

        XT_AT, GATE_AT, SCORE_AT = 3, 4, 5
        VEC_HEAD = 5
        VEC_LAYER = 4 + H * VEC_HEAD + 1
        VEC_GRAPH = 6 + 2 * VEC_LAYER
        ROUTE_STEPS = 2 * TH + 5 + 6

        def turned_bank(b):
            return bank[:, b, 0:N].bitcast(BF16).rearrange("p (c n) -> p c n", c=C)

        def h1_hi_part(act, k):
            half, c = k // C, k % C
            act.wait_ge(h1_rdy, k + 1)
            nc.scalar.copy(h1_hi[:, c, tok(half)], h1[:, c, tok(half)]).then_inc(h1_hi_rdy, 1)

        def act_experts(act, run):
            def xt_part(half):
                for c in range(C):
                    act.wait_ge(xt_mm, (run * HALVES + half) * C + c + 1)
                    nc.scalar.copy(xt_hi[:, c, tok(half)], bank[:, XT[c], :]).then_inc(xt_hi_rdy, 1)

            def gate_tanh(half):
                n = run * HALVES + half + 1
                act.wait_ge(gate_in_rdy, n)
                nc.scalar.activation(gate_h[:], gate_in[:], ACT.Tanh).then_inc(gate_h_rdy, 1)

            def diff_tanh(half):
                n = run * HALVES + half + 1
                act.wait_ge(ldiff_rdy, n)
                nc.scalar.activation(lth[:], ldiff[:], ACT.Tanh, scale=0.5).then_inc(lth_rdy, 1)

            xt_part(0)
            gate_tanh(0)
            diff_tanh(0)
            for k in range(HALVES * E):
                n = run * HALVES * E + k
                e = k % E
                act.wait_ge(up_mm, n + 1)
                if n >= 2:
                    act.wait_ge(hid_rdy, n - 1)
                nc.scalar.activation(act_out[:, n % 2, :], bank[:, UP[n % 2], :], ACT.Silu,
                                     bias=bup_sb[:, e:e + 1]).then_inc(silu_rdy, 1)
                act.wait_ge(hid_rdy, n + 1)
                if n >= SLOTS:
                    act.wait_ge(down_mm, n - SLOTS + 1)
                nc.scalar.copy(hid_hi[:, n % SLOTS, :], hid[:, n % 2, :]).then_inc(hid_hi_rdy, 1)
                if k == XT_AT:
                    xt_part(1)
                if k == GATE_AT:
                    gate_tanh(1)
                if k == SCORE_AT:
                    diff_tanh(1)

        def pe_experts(pe, run):
            def xt_part(half):
                pe.wait_ge(const_rdy, 2)
                pe.wait_ge(xn_rdy, NT * run + TH * (half + 1))
                if run * HALVES + half >= 1:
                    pe.wait_ge(xt_lo_rdy, (run * HALVES + half) * C)
                for c in range(C):
                    for t in range(TH):
                        mm = nc.tensor.transpose(bank[:, XT[c], t * P:(t + 1) * P],
                                                 xn[:, half * TH + t, c * P:(c + 1) * P], ident[:])
                    mm.then_inc(xt_mm, 1)

            def gate_part(half):
                pe.wait_ge(wg1_rdy, 2)
                pe.wait_ge(xt_lo_rdy, (run * HALVES + half + 1) * C)
                pe.wait_ge(xt_hi_rdy, (run * HALVES + half + 1) * C)
                for t in range(TH):
                    rows = slice((half * TH + t) * P, (half * TH + t + 1) * P)
                    for c in range(C):
                        nc.tensor.matmul(bank[:, ROUTE, t * 2 * E:(t + 1) * 2 * E], xt_hi[:, c, rows], wg1_parts[:, c, :],
                                         start=(c == 0), stop=False)
                        mm = nc.tensor.matmul(bank[:, ROUTE, t * 2 * E:(t + 1) * 2 * E], xt_lo[:, c, rows],
                                              wg1_parts[:, c, :], start=False, stop=(c == C - 1))
                mm.then_inc(gate_mm, 1)

            def score_part(half):
                pe.wait_ge(score_rdy, 2 * (run * HALVES + half + 1))
                for t in range(TH):
                    mm = nc.tensor.transpose(bank[0:2 * E, ROUTE, t * P:(t + 1) * P], score_parts[:, t, :], ident[:])
                mm.then_inc(score_mm, 1)

            def up(k):
                n = run * HALVES * E + k
                half, e = k // E, k % E
                cols = slice(e * HE, (e + 1) * HE)
                if n >= 2:
                    pe.wait_ge(silu_rdy, n - 1)
                if k == 0:
                    pe.wait_ge(wup_rdy, 2 * C)
                    pe.wait_ge(exp1_rdy, NT // 2)
                    pe.wait_ge(elu1_rdy, NT // 2)
                dst = bank[:, UP[n % 2], :]
                for c in range(C):
                    nc.tensor.matmul(dst, wup_hi[:, c, cols], xt_hi[:, c, tok(half)], start=(c == 0), stop=False)
                    nc.tensor.matmul(dst, wup_lo[:, c, cols], xt_hi[:, c, tok(half)], start=False, stop=False)
                    mm = nc.tensor.matmul(dst, wup_hi[:, c, cols], xt_lo[:, c, tok(half)], start=False, stop=(c == C - 1))
                mm.then_inc(up_mm, 1)

            def spread(k):
                n = run * HALVES * E + k
                half, e = k // E, k % E
                if e == 0:
                    pe.wait_ge(score_t_rdy, run * HALVES + half + 1)
                if k == 0:
                    pe.wait_ge(pick_rdy, 1)
                if n >= 1:
                    pe.wait_ge(hid_rdy, n)
                nc.tensor.matmul(bank[:, PICK, :], pick[:, e, :], score_t[:, tok(half)], start=True, stop=True).then_inc(pick_mm, 1)

            def down(k):
                n = run * HALVES * E + k
                half, e = k // E, k % E
                if k == 0:
                    pe.wait_ge(bdown_rdy, 2)
                    pe.wait_ge(wdown_rdy, 4)
                if e == 0 and run * HALVES + half >= 1:
                    pe.wait_ge(out_rdy, (run * HALVES + half) * TH)
                pe.wait_ge(hid_hi_rdy, n + 1)
                pe.wait_ge(hid_lo_rdy, n + 1)
                for t in range(TH):
                    dst = bank[:, DOWN[t // 2], (t % 2) * D:(t % 2 + 1) * D]
                    if e == 0:
                        rows = slice((half * TH + t) * P, (half * TH + t + 1) * P)
                        nc.tensor.matmul(dst, score_t[:, rows], bdown_hi[:], start=(t % 2 == 0), stop=False, skip_group_check=True)
                        nc.tensor.matmul(dst, score_t[:, rows], bdown_lo[:], start=False, stop=False, skip_group_check=True)
                    part = slice(t * P, (t + 1) * P)
                    nc.tensor.matmul(dst, hid_hi[:, n % SLOTS, part], wdown_hi[:, e, :], start=False, stop=False, skip_group_check=True)
                    nc.tensor.matmul(dst, hid_hi[:, n % SLOTS, part], wdown_lo[:, e, :], start=False, stop=False, skip_group_check=True)
                    mm = nc.tensor.matmul(dst, hid_lo[:, n % SLOTS, part], wdown_hi[:, e, :], start=False,
                                          stop=(e == E - 1), skip_group_check=True)
                mm.then_inc(down_mm, 1)

            xt_part(0)
            gate_part(0)
            up(0)
            up(1)
            score_part(0)
            spread(0)
            for k in range(1, HALVES * E + LAG):
                if 2 <= k < HALVES * E:
                    up(k)
                if k == XT_AT:
                    xt_part(1)
                if k == GATE_AT:
                    gate_part(1)
                if k == SCORE_AT + 1:
                    score_part(1)
                if k < HALVES * E:
                    spread(k)
                if k >= LAG:
                    down(k - LAG)

        def dve_experts(dve, run, elu1, check_peaks, check_rows, check_flag):
            r0 = run * HALVES

            def rows_stats(half):
                for t in range(half * TH, (half + 1) * TH):
                    nc.vector.bn_stats(stat[:, t, :], xa[:, t, :]).then_inc(stat_rdy, 1)
                for t in range(half * TH, (half + 1) * TH):
                    dve.wait_ge(stat_rdy, NT * run + t + 1)
                    nc.vector.bn_aggr(mv[:, t, :], stat[:, t, :]).then_inc(mv_rdy, 1)

            def rows_norm(half):
                dve.wait_ge(rstd_rdy, r0 + half + 1)
                dve.wait_ge(mv_rdy, NT * run + TH * (half + 1))
                for t in range(half * TH, (half + 1) * TH):
                    nc.vector.tensor_scalar(xn[:, t, :], xa[:, t, :], mv[:, t, 0:1], rstd[:, t:t + 1],
                                            ALU.subtract, ALU.mult).then_inc(xn_rdy, 1)

            def xt_part(half):
                for c in range(C):
                    dve.wait_ge(xt_hi_rdy, (r0 + half) * C + c + 1)
                    nc.vector.tensor_tensor(xt_lo[:, c, tok(half)], bank[:, XT[c], :], xt_hi[:, c, tok(half)].bitcast(F32),
                                            ALU.subtract).then_inc(xt_lo_rdy, 1)

            def per_expert(ap):
                return ap.broadcast_to([P, TH, E])

            def gate_sum(half):
                n = r0 + half
                dve.wait_ge(gate_mm, n + 1)
                nc.vector.tensor_reduce(gate_in[:], bank[:, ROUTE, 0:TH * 2 * E].rearrange("p (t k e) -> p t e k", t=TH, k=2),
                                        AX.X, ALU.add).then_inc(gate_in_rdy, 1)

            def gate_logits(half):
                n = r0 + half
                base = [n * ROUTE_STEPS]

                def link(ins, chained=True):
                    base[0] += 1
                    ins.then_inc(route_step, 1)
                    if chained:
                        dve.wait_ge(route_step, base[0])

                dve.wait_ge(gate_h_rdy, n + 1)
                link(nc.vector.tensor_tensor(gate_prod[:], gate_h[:].rearrange("p t (a k) -> p t a k", a=1).broadcast_to([P, TH, E, E]),
                                             wg2_sb[:].rearrange("p (a e) k -> p a e k", a=1).broadcast_to([P, TH, E, E]), ALU.mult))
                link(nc.vector.tensor_reduce(logits[:], gate_prod[:], AX.X, ALU.add))
                for t in range(TH):
                    link(nc.vector.max(ltop[:, t, :], logits[:, t, :]), t == TH - 1)
                nc.vector.tensor_tensor(ldiff[:], ltop[:, :, 0], ltop[:, :, 1], ALU.subtract).then_inc(ldiff_rdy, 1)
                for t in range(TH):
                    link(nc.vector.max_index(lidx[:, t, :], ltop[:, t, :], logits[:, t, :]), t == TH - 1)
                link(nc.vector.tensor_copy(lidx_f[:], lidx[:]))
                for r in range(2):
                    link(nc.vector.tensor_tensor(hit[:, r, :, :], expert_no[:], per_expert(lidx_f[:, :, r:r + 1]), ALU.is_equal), r == 1)
                assert base[0] == n * ROUTE_STEPS + 2 * TH + 5

            def gate_scores(half):
                n = r0 + half
                base = [n * ROUTE_STEPS + 2 * TH + 5]

                def link(ins, chained=True):
                    base[0] += 1
                    ins.then_inc(route_step, 1)
                    if chained:
                        dve.wait_ge(route_step, base[0])

                dve.wait_ge(lth_rdy, n + 1)
                link(nc.vector.tensor_scalar(prob[:, 0, :], lth[:], 0.5, 0.5, ALU.mult, ALU.add), False)
                link(nc.vector.tensor_scalar(prob[:, 1, :], lth[:], -0.5, 0.5, ALU.mult, ALU.add))
                for r in range(2):
                    link(nc.vector.tensor_tensor(score_k[:, r, :, :], hit[:, r, :, :],
                                                 per_expert(prob[:, r, :].rearrange("p (t a) -> p t a", a=1)), ALU.mult), r == 1)
                link(nc.vector.tensor_tensor(score[:], score_k[:, 0, :, :], score_k[:, 1, :, :], ALU.add))
                if n >= 1:
                    dve.wait_ge(score_mm, n)
                link(nc.vector.tensor_copy(score_hi[:], score[:]))
                nc.vector.tensor_copy(score_parts[:, :, 0:E], score_hi[:].bitcast(F32)).then_inc(score_rdy, 1)
                nc.vector.tensor_tensor(score_parts[:, :, E:2 * E], score[:], score_hi[:].bitcast(F32), ALU.subtract).then_inc(score_rdy, 1)
                assert base[0] == (n + 1) * ROUTE_STEPS

            def scores_turned(half):
                n = r0 + half
                dve.wait_ge(score_mm, n + 1)
                nc.vector.tensor_copy(score_t[:, tok(half)], bank[0:2 * E, ROUTE, :]).then_inc(score_t_rdy, 1)

            def weigh(k):
                n = r0 * E + k
                dve.wait_ge(silu_rdy, n + 1)
                dve.wait_ge(pick_mm, n + 1)
                if n >= 2:
                    dve.wait_ge(hid_hi_rdy, n - 1)
                    dve.wait_ge(hid_lo_rdy, n - 1)
                nc.vector.tensor_tensor(hid[:, n % 2, :], act_out[:, n % 2, :], bank[:, PICK, :], ALU.mult).then_inc(hid_rdy, 1)

            def weigh_lo(k):
                n = r0 * E + k
                dve.wait_ge(hid_hi_rdy, n + 1)
                if n >= SLOTS:
                    dve.wait_ge(down_mm, n - SLOTS + 1)
                nc.vector.tensor_tensor(hid_lo[:, n % SLOTS, :], hid[:, n % 2, :], hid_hi[:, n % SLOTS, :].bitcast(F32),
                                        ALU.subtract).then_inc(hid_lo_rdy, 1)

            def finish(half):
                dve.wait_ge(down_mm, r0 * E + E * (half + 1))
                if run == 1 and half == 0:
                    dve.wait_ge(stored, 16 * (NT // 2))
                for t in range(TH):
                    nc.vector.scalar_tensor_tensor(out=out_sb[:, half * TH + t, :],
                                                   in0=bank[:, DOWN[t // 2], (t % 2) * D:(t % 2 + 1) * D],
                                                   scalar=gates[:, 1:2], in1=xa[:, half * TH + t, :],
                                                   op0=ALU.mult, op1=ALU.add).then_inc(out_rdy, 1)

            first = run == 0
            rows_stats(0)
            if first:
                elu1(2)
            rows_norm(0)
            xt_part(0)
            if first:
                elu1(3)
            gate_sum(0)
            rows_stats(1)
            gate_logits(0)
            gate_scores(0)
            scores_turned(0)
            for k in range(HALVES * E):
                weigh(k)
                if k == 0:
                    rows_norm(1)
                weigh_lo(k)
                if k == XT_AT:
                    xt_part(1)
                if k == GATE_AT:
                    gate_sum(1)
                    gate_logits(1)
                if k == SCORE_AT:
                    gate_scores(1)
                if k == SCORE_AT + 1:
                    scores_turned(1)
                if first and k == 2:
                    check_peaks()
                if first and k == SCORE_AT + 2 + 2:
                    check_rows()
                if first and k == HALVES * E - 1:
                    check_flag()
                if k == E + LAG - 1:
                    finish(0)
            finish(1)

        def on_general(eng, body):
            eng.wait_ge(flag_rdy, 1)
            v = eng.value_load(flag[0:1, 0:1])
            with eng.If(v != 0):
                body()
            with eng.Else():
                eng.wait_ge(flag_rdy, 1)
            eng.wait_ge(flag_rdy, 1)

        @block.sync
        def _(sp):
            for b in range(B):
                sp.dma_start(x_sb[:, pair(b), :], x[b].rearrange("(c p) d -> p c d", p=P)).then_inc(x_in[b], 16)
            sp.dma_start(w1_sb[:], w1.rearrange("(c p) n -> p c n", p=P)).then_inc(w1_ld, 16)
            sp.dma_start(wup_sb[:], wup.rearrange("(c p) n -> p c n", p=P)).then_inc(wup_ld, 16)
            sp.dma_start(wdown_sb[:], wdown.rearrange("e p n -> p e n")).then_inc(wdown_ld, 16)
            sp.dma_start(bdown_sb[0:E, :], bdown).then_inc(bdown_ld, 16)
            sp.dma_start(bdown_sb[E:2 * E, :], bdown).then_inc(bdown_ld, 16)
            sp.dma_start(w0t_sb[:], w0_t.rearrange("(c p) n -> p c n", p=P)).then_inc(check_ld, 16)
            sp.dma_start(w1t_sb[:], w1_t.rearrange("(c p) n -> p c n", p=P)).then_inc(check_ld, 16)
            sp.dma_start(a_sb[:], avec.rearrange("k h o -> h k o")).then_inc(check_ld, 16)

            def store(run):
                for q in range(NT // 2):
                    sp.wait_ge(out_rdy, NT * run + 2 * q + 2)
                    sp.dma_start(out[q].rearrange("(c p) d -> p c d", p=P), out_sb[:, pair(q), :]).then_inc(stored, 16)
                sp.wait_ge(stored, 16 * (NT // 2) * (run + 1))

            store(0)

            def general():
                sp.dma_start(b_bc[:, 0, :], b0_r.broadcast_to([P, H * FO])).then_inc(g_bc_ld, 16)
                sp.dma_start(b_bc[:, 1, :], b1_r.broadcast_to([P, H * FO])).then_inc(g_bc_ld, 16)
                for k in range(4):
                    sp.dma_start(a_bc[k][:, 0, :], avec[k].rearrange("h o -> (h o)").rearrange("(a n) -> a n", a=1)
                                 .broadcast_to([P, H * FO])).then_inc(g_bc_ld, 16)
                with sp.Fori(0, B) as b:
                    sp.wait_ge(g_xa, b + 1)
                    sp.dma_start(ctxt_b, ctx_t[:, bass.ds(b * N, N)]).then_inc(g_graph_ld, 16)
                store(1)

            on_general(sp, general)

        @block.gpsimd
        def _(pool):
            nc.gpsimd.memset(ident_bf[:], 0.0).then_inc(const_raw, 1)
            nc.gpsimd.memset(ident[:], 0.0).then_inc(const_raw, 1)
            pool.wait_ge(const_raw, 2)
            nc.gpsimd.affine_select(out=ident_bf[:], in_=ident_bf[:], compare_op=ALU.not_equal, fill=1.0, base=0,
                                    pattern=[[-1, P]], channel_multiplier=1).then_inc(const_rdy, 1)
            pool.wait_ge(w0_ld, 32)
            nc.gpsimd.tensor_copy(w0_hi[:], w0_sb[:]).then_inc(small_rdy, 1)
            nc.gpsimd.affine_select(out=ident[:], in_=ident[:], compare_op=ALU.not_equal, fill=1.0, base=0,
                                    pattern=[[-1, P]], channel_multiplier=1).then_inc(const_rdy, 1)
            pool.wait_ge(small_rdy, 1)
            nc.gpsimd.tensor_tensor(w0_lo[:], w0_sb[:], w0_hi[:].bitcast(F32), ALU.subtract).then_inc(w0_rdy, 1)
            pool.wait_ge(w1_ld, 16)
            nc.gpsimd.tensor_copy(w1_hi[:], w1_sb[:]).then_inc(small_rdy, 1)
            nc.gpsimd.memset(ones[:], 1.0).then_inc(ones_rdy, 1)
            nc.gpsimd.memset(half_power[:], -0.5).then_inc(ones_rdy, 1)
            pool.wait_ge(small_rdy, 2)
            nc.gpsimd.tensor_tensor(w1_lo[:], w1_sb[:], w1_hi[:].bitcast(F32), ALU.subtract).then_inc(w1_rdy, 1)
            pool.wait_ge(wup_ld, 16)
            for c in range(C):
                nc.gpsimd.tensor_copy(wup_hi[:, c, :], wup_sb[:, c, :]).then_inc(wup_rdy, 1)
            for c in range(C):
                pool.wait_ge(wup_rdy, 1 + c)
                nc.gpsimd.tensor_tensor(wup_lo[:, c, :], wup_sb[:, c, :], wup_hi[:, c, :].bitcast(F32),
                                        ALU.subtract).then_inc(wup_rdy, 1)
            nc.gpsimd.memset(pick_f, 0.0).then_inc(const_raw, 1)
            pool.wait_ge(const_raw, 3)
            nc.gpsimd.affine_select(out=pick_f, in_=pick_f, compare_op=ALU.not_equal, fill=1.0, base=0,
                                    pattern=[[-1, E], [0, P]], channel_multiplier=1).then_inc(const_raw, 1)
            pool.wait_ge(const_raw, 4)
            nc.gpsimd.affine_select(out=pick_f, in_=pick_f, compare_op=ALU.not_equal, fill=1.0, base=-E,
                                    pattern=[[-1, E], [0, P]], channel_multiplier=1).then_inc(const_raw, 1)
            nc.gpsimd.iota(expert_no[:], pattern=[[0, TH], [1, E]], base=0, channel_multiplier=0,
                           allow_small_or_imprecise_dtypes=True).then_inc(const_raw, 1)
            pool.wait_ge(const_raw, 5)
            nc.gpsimd.tensor_copy(pick[:], pick_f).then_inc(pick_rdy, 1)

            def row_power(run, half):
                n = HALVES * run + half + 1
                pool.wait_ge(mv_rdy, (half + 1) * TH + NT * run)
                pool.wait_ge(ones_rdy, 2)
                nc.gpsimd.tensor_scalar(veps[:, tiles(half)], mv[:, tiles(half), 1], EPS, None, ALU.add).then_inc(veps_rdy, 1)
                pool.wait_ge(veps_rdy, n)
                nc.gpsimd.tensor_tensor(rstd[:, tiles(half)], veps[:, tiles(half)], half_power[:, 0:TH],
                                        ALU.pow).then_inc(rstd_rdy, 1)

            row_power(0, 0)
            pool.wait_ge(wdown_ld, 16)
            for c in range(2):
                nc.gpsimd.tensor_copy(wdown_hi[:, c * 4:c * 4 + 4, :], wdown_sb[:, c * 4:c * 4 + 4, :]).then_inc(wdown_rdy, 1)
                pool.wait_ge(wdown_rdy, 2 * c + 1)
                nc.gpsimd.tensor_tensor(wdown_lo[:, c * 4:c * 4 + 4, :], wdown_sb[:, c * 4:c * 4 + 4, :],
                                        wdown_hi[:, c * 4:c * 4 + 4, :].bitcast(F32), ALU.subtract).then_inc(wdown_rdy, 1)
            row_power(0, 1)

            pool.wait_ge(peaks_rdy, 1)
            nc.gpsimd.partition_all_reduce(peaks_all[:], peaks[:], P, bass.bass_isa.ReduceOp.max).then_inc(peaks_all_rdy, 1)
            pool.wait_ge(peaks_all_rdy, 1)
            pa = peaks_all

            steps = [0]

            def then_step(ins):
                steps[0] += 1
                ins.then_inc(pool_step, 1)
                pool.wait_ge(pool_step, steps[0])

            then_step(nc.gpsimd.tensor_tensor(bound[:, 0:1], pa[:, 0:1], pa[:, 1:2], ALU.mult))
            then_step(nc.gpsimd.tensor_tensor(bound[:, 1:2], pa[:, 3:4], pa[:, 4:5], ALU.add))
            then_step(nc.gpsimd.tensor_tensor(bound[:, 2:3], pa[:, 5:6], pa[:, 6:7], ALU.add))
            then_step(nc.gpsimd.tensor_tensor(bound[:, 3:4], bound[:, 0:1], pa[:, 7:8], ALU.add))
            then_step(nc.gpsimd.tensor_scalar(bound[:, 3:4], bound[:, 3:4], 1.0, None, ALU.max))
            then_step(nc.gpsimd.tensor_tensor(bound[:, 3:4], bound[:, 3:4], pa[:, 2:3], ALU.mult))
            then_step(nc.gpsimd.tensor_tensor(bound[:, 3:4], bound[:, 3:4], bound[:, 2:3], ALU.mult))
            then_step(nc.gpsimd.tensor_tensor(bound[:, 4:5], bound[:, 0:1], bound[:, 1:2], ALU.mult))
            then_step(nc.gpsimd.tensor_tensor(bound[:, 5:6], bound[:, 3:4], bound[:, 4:5], ALU.add))
            then_step(nc.gpsimd.tensor_scalar(bound[:, 6:7], bound[:, 5:6], 3.0 / MASK, 200.0 / MASK + 2e-6, ALU.mult, ALU.add))
            pool.wait_ge(xstat_rdy, 2 * NT)
            then_step(nc.gpsimd.tensor_scalar(xrstd[:], xmv[:, :, 1], EPS, None, ALU.add))
            then_step(nc.gpsimd.tensor_tensor(xrstd[:], xrstd[:], half_power[:], ALU.pow))
            then_step(nc.gpsimd.tensor_tensor(lead[:], top[:, :, 0], top[:, :, 1], ALU.subtract))
            then_step(nc.gpsimd.tensor_tensor(lead[:], lead[:], xrstd[:], ALU.mult))
            then_step(nc.gpsimd.tensor_tensor(need[:], top[:, :, 0], xmv[:, :, 0], ALU.subtract))
            then_step(nc.gpsimd.tensor_tensor(need[:], need[:], xrstd[:], ALU.mult))
            then_step(nc.gpsimd.tensor_scalar(need[:], need[:], 2e-6, bound[:, 6:7], ALU.mult, ALU.add))
            then_step(nc.gpsimd.tensor_tensor(spare[:], lead[:], need[:], ALU.subtract))
            then_step(nc.gpsimd.tensor_scalar(good[:], spare[:], 0.0, None, ALU.is_gt))
            nc.gpsimd.partition_all_reduce(good_all[:], good[:], P, bass.bass_isa.ReduceOp.add).then_inc(good_rdy, 1)

            def general():
                row_power(1, 0)
                row_power(1, 1)

            on_general(pool, general)

        @block.scalar
        def _(act):
            act.dma_start(ctx_sb[:], ctx_in.rearrange("b (c p) k -> p (b c) k", p=P)).then_inc(ctx_ld, 16)
            act.dma_start(w0_sb[0:FIN, :], w0).then_inc(w0_ld, 16)
            act.dma_start(w0_sb[FIN:P, :], w0).then_inc(w0_ld, 16)
            act.dma_start(b0_sb[:], b0_c).then_inc(small_ld, 16)
            act.dma_start(gates[:], g2.broadcast_to([P, 2])).then_inc(small_ld, 16)
            act.dma_start(bup_sb[:], bup_c).then_inc(small_ld, 16)
            act.dma_start(b1_sb[0:1, :], b1_r).then_inc(b1_ld, 16)
            act.dma_start(b1_sb[32:33, :], b1_r).then_inc(b1_ld, 16)
            act.dma_start(wg1_sb[:], wg1.rearrange("(c p) e -> p c e", p=P)).then_inc(gate_ld, 16)
            act.dma_start(wg2_sb[:], wg2_r.broadcast_to([P, E * E]).rearrange("p (a b) -> p a b", a=E)).then_inc(gate_ld, 16)
            act.wait_ge(ctx_ld, 16)
            nc.scalar.copy(ctx_parts[:, :, 0:FIN], ctx_sb[:]).then_inc(ctx_hi_rdy, 1)
            act.wait_ge(small_ld, 48)
            nc.scalar.activation(gates[:], gates[:], ACT.Tanh).then_inc(gates_rdy, 1)
            for b in range(B):
                act.wait_ge(turned, b + 1)
                nc.scalar.copy(onehot_t[:, b, :, :], turned_bank(b)).then_inc(onehot_t_rdy, 1)
            for b in range(B):
                act.wait_ge(twice_mm, b + 1)
                nc.scalar.copy(twice[:, b * N:(b + 1) * N], bank[:, 6 + b % 2, 0:N]).then_inc(twice_rdy, 1)
            for k in range(HALVES * C):
                half, c = k // C, k % C
                act.wait_ge(feat0_mm, k + 1)
                nc.scalar.activation(exp0[:, c, tok(half)], bank[:, k, :], ACT.Exp, bias=b0_sb[:, c:c + 1]).then_inc(exp0_rdy, 1)
                if k >= 1:
                    h1_hi_part(act, k - 1)
            h1_hi_part(act, HALVES * C - 1)
            for q in range(NT // 2):
                act.wait_ge(feat1_mm, q + 1)
                nc.scalar.activation(exp1[:, pair(q), :], bank[:, 4 + q, :], ACT.Exp).then_inc(exp1_rdy, 1)
            act_experts(act, 0)

            def general():
                with act.Fori(0, B) as b:
                    act.wait_ge(g_vec, b * VEC_GRAPH + 1)
                    nc.scalar.activation(grstd[:], gve[:], ACT.Sqrt).then_inc(g_sqrt, 1)
                    for l in range(2):
                        act.wait_ge(g_feat_mm, b * 2 + (l + 1))
                        nc.scalar.copy(feat, bank[:, 0, :]).then_inc(g_feat, 1)
                        with act.Fori(0, H) as h:
                            turn = b * (2 * H) + h + (l * H + 1)
                            act.wait_ge(g_max, turn)
                            for c in range(C):
                                nc.scalar.activation(pr[:, c, :], sc2[:, c, :], ACT.Exp, bias=nmax[:, c:c + 1],
                                                     accum_out=psum_p[:, c:c + 1]).then_inc(g_exp, 1)
                            act.wait_ge(g_alpha_mm, turn)
                            nc.scalar.copy(alpha_t, bank[:, 2, :]).then_inc(g_alpha_t, 1)
                        act.wait_ge(g_z, b * 2 + (l + 1))
                        nc.scalar.activation(gexp, gz, ACT.Exp).then_inc(g_zexp, 1)
                        if l == 0:
                            act.wait_ge(g_h_mm, b + 1)
                            nc.scalar.copy(gh_t, bank[:, 4, :]).then_inc(g_h_t, 1)
                act_experts(act, 1)

            on_general(act, general)


        @block.tensor
        def _(pe):
            pe.wait_ge(const_rdy, 1)
            for b in range(B):
                pe.wait_ge(onehot_rdy, 2 * b + 2)
                for i in range(C):
                    for j in range(C):
                        mm = nc.tensor.transpose(turned_bank(b)[:, j, i * P:(i + 1) * P],
                                                 onehot[:, 2 * b + i, j * P:(j + 1) * P], ident_bf[:])
                mm.then_inc(turned, 1)
            pe.wait_ge(ctx_rdy, 1)
            for b in range(B):
                pe.wait_ge(onehot_t_rdy, b + 1)
                if b >= 2:
                    pe.wait_ge(once_rdy, b - 1)
                for i in range(C):
                    for j in range(C):
                        mm = nc.tensor.matmul(bank[:, 4 + b % 2, i * P:(i + 1) * P],
                                              onehot_t[:, b, j, i * P:(i + 1) * P], ctx_parts[:, 2 * b + j, :],
                                              start=(j == 0), stop=(j == C - 1))
                mm.then_inc(once_mm, 1)
            for b in range(B):
                pe.wait_ge(once_rdy, b + 1)
                if b >= 2:
                    pe.wait_ge(twice_rdy, b - 1)
                for j in range(C):
                    mm = nc.tensor.matmul(bank[:, 6 + b % 2, 0:N], once[:, b, j, :], onehot_t[:, b, j, :],
                                          start=(j == 0), stop=(j == C - 1))
                mm.then_inc(twice_mm, 1)
            pe.wait_ge(w0_rdy, 1)
            for half in range(HALVES):
                pe.wait_ge(twice_rdy, 2 * half + 2)
                for c in range(C):
                    k = half * C + c
                    nc.tensor.matmul(bank[:, k, :], w0_hi[:, c * P:(c + 1) * P], twice[:, tok(half)], start=True, stop=False)
                    nc.tensor.matmul(bank[:, k, :], w0_lo[:, c * P:(c + 1) * P], twice[:, tok(half)],
                                     start=False, stop=True).then_inc(feat0_mm, 1)
            pe.wait_ge(w1_rdy, 1)
            pe.wait_ge(b1_rdy, 4)
            pe.wait_ge(once_rdy, B)
            for t in range(NT):
                half = t // TH
                if t % TH == 0:
                    pe.wait_ge(h1_lo_rdy, C * (half + 1))
                    pe.wait_ge(h1_hi_rdy, C * (half + 1))
                dst = bank[:, 4 + t // 2, (t % 2) * D:(t % 2 + 1) * D]
                nc.tensor.matmul(dst, ones_r[:], b1_parts[:], start=True, stop=False)
                for c in range(C):
                    rows = slice(t * P, (t + 1) * P)
                    nc.tensor.matmul(dst, h1_hi[:, c, rows], w1_hi[:, c, :], start=False, stop=False)
                    nc.tensor.matmul(dst, h1_hi[:, c, rows], w1_lo[:, c, :], start=False, stop=False)
                    mm = nc.tensor.matmul(dst, h1_lo[:, c, rows], w1_hi[:, c, :], start=False, stop=(c == C - 1))
                if t % 2 == 1:
                    mm.then_inc(feat1_mm, 1)
            pe_experts(pe, 0)

            def general():
                with pe.Fori(0, B) as b:
                    for l in range(2):
                        if l == 0:
                            pe.wait_ge(g_graph_ld, b * 16 + 16)
                        else:
                            pe.wait_ge(g_h_t, b + 1)
                        for j in range(C):
                            dst = bank[:, 0, j * D:(j + 1) * D]
                            if l == 0:
                                mm = nc.tensor.matmul(dst, ctxt_b[:, j * P:(j + 1) * P], w0_sb[0:FIN, :], start=True, stop=True)
                            else:
                                for c in range(C):
                                    mm = nc.tensor.matmul(dst, gh_t[:, c, j * P:(j + 1) * P], w1_sb[:, c, :],
                                                          start=(c == 0), stop=(c == C - 1))
                        mm.then_inc(g_feat_mm, 1)
                        with pe.Fori(0, H) as h:
                            turn = b * (2 * H) + h + (l * H + 1)
                            pe.wait_ge(g_diag, turn)
                            for j in range(C):
                                mm = nc.tensor.matmul(bank[:, 1, j * P:(j + 1) * P], ones[:], diag[:, j, :],
                                                      start=True, stop=True)
                            mm.then_inc(g_row_mm, 1)
                            pe.wait_ge(g_alpha, turn * 2)
                            for i in range(C):
                                for j in range(C):
                                    mm = nc.tensor.transpose(bank[:, 2, j * N + i * P:j * N + (i + 1) * P],
                                                             alpha[:, i, j * P:(j + 1) * P], ident[:])
                            mm.then_inc(g_alpha_mm, 1)
                            pe.wait_ge(g_alpha_t, turn)
                            for i in range(C):
                                for j in range(C):
                                    mm = nc.tensor.matmul(bank[:, 3, bass.ds(h * FO + i * D, FO)],
                                                          alpha_t[:, j, i * P:(i + 1) * P],
                                                          feat[:, j, bass.ds(h * FO, FO)],
                                                          start=(j == 0), stop=(j == C - 1))
                            mm.then_inc(g_out_mm, 1)
                        if l == 0:
                            pe.wait_ge(g_h, b * 2 + 1)
                            for i in range(C):
                                for c in range(C):
                                    mm = nc.tensor.transpose(bank[:, 4, c * N + i * P:c * N + (i + 1) * P],
                                                             gh[:, i, c * P:(c + 1) * P], ident[:])
                            mm.then_inc(g_h_mm, 1)
                pe_experts(pe, 1)

            on_general(pe, general)

        @block.vector
        def _(dve):
            nc.vector.memset(b1_parts[:].bitcast(F32), 0.0).then_inc(b1_rdy, 1)
            nc.vector.memset(ones_r[:].bitcast(F32), 1.0).then_inc(b1_rdy, 1)
            nc.vector.memset(peaks[:], 0.0).then_inc(peaks_part, 1)
            dve.wait_ge(ctx_hi_rdy, 1)
            nc.vector.tensor_tensor(ctx_parts[:, :, FIN:2 * FIN], ctx_sb[:], ctx_parts[:, :, 0:FIN].bitcast(F32),
                                    ALU.subtract).then_inc(ctx_rdy, 1)
            for t in range(NT):
                if t % 2 == 0:
                    dve.wait_ge(x_in[t // 2], 16)
                nc.vector.max(top[:, t, :], x_sb[:, t, :]).then_inc(top_rdy, 1)
                if t % 2 == 1:
                    for s in (t - 1, t):
                        dve.wait_ge(top_rdy, s + 1)
                        nc.vector.tensor_scalar(onehot[:, s, :], x_sb[:, s, :], top[:, s, 0:1], None,
                                                ALU.is_equal).then_inc(onehot_rdy, 1)
            for b in range(B):
                dve.wait_ge(once_mm, b + 1)
                nc.vector.tensor_copy(once[:, b, :, :], bank[:, 4 + b % 2, 0:N].rearrange("p (c n) -> p c n", c=C)
                                      ).then_inc(once_rdy, 1)
            dve.wait_ge(b1_ld, 32)
            dve.wait_ge(b1_rdy, 2)
            nc.vector.tensor_copy(b1_parts[0:1, :], b1_sb[0:1, :]).then_inc(b1_rdy, 1)
            nc.vector.tensor_copy(b1_hi[32:33, :], b1_sb[32:33, :]).then_inc(bdown_rdy, 1)
            dve.wait_ge(bdown_rdy, 1)
            nc.vector.tensor_tensor(b1_parts[32:33, :], b1_sb[32:33, :], b1_hi[32:33, :].bitcast(F32),
                                    ALU.subtract).then_inc(b1_rdy, 1)
            dve.wait_ge(small_ld, 48)

            def h1_lo_part(k):
                half, c = k // C, k % C
                dve.wait_ge(h1_hi_rdy, k + 1)
                nc.vector.tensor_tensor(h1_lo[:, c, tok(half)], h1[:, c, tok(half)], h1_hi[:, c, tok(half)].bitcast(F32),
                                        ALU.subtract).then_inc(h1_lo_rdy, 1)

            for k in range(HALVES * C):
                half, c = k // C, k % C
                dve.wait_ge(exp0_rdy, k + 1)
                nc.vector.tensor_scalar(exp0[:, c, tok(half)], exp0[:, c, tok(half)], 1.0, -1.0, ALU.min, ALU.add).then_inc(elu0_part, 1)
                dve.wait_ge(elu0_part, k + 1)
                nc.vector.scalar_tensor_tensor(out=h1[:, c, tok(half)], in0=bank[:, k, :], scalar=b0_sb[:, c:c + 1],
                                               in1=exp0[:, c, tok(half)], op0=ALU.add, op1=ALU.max).then_inc(h1_rdy, 1)
                if k >= 1:
                    h1_lo_part(k - 1)
            h1_lo_part(HALVES * C - 1)

            dve.wait_ge(gate_ld, 32)
            nc.vector.tensor_copy(wg1_parts[:, :, 0:E], wg1_sb[:]).then_inc(wg1_rdy, 1)
            dve.wait_ge(bdown_ld, 32)
            nc.vector.tensor_copy(bdown_hi[:], bdown_sb[:]).then_inc(bdown_rdy, 1)
            dve.wait_ge(wg1_rdy, 1)
            nc.vector.tensor_tensor(wg1_parts[:, :, E:2 * E], wg1_sb[:], wg1_parts[:, :, 0:E].bitcast(F32),
                                    ALU.subtract).then_inc(wg1_rdy, 1)
            dve.wait_ge(bdown_rdy, 2)
            nc.vector.tensor_tensor(bdown_lo[:], bdown_sb[:], bdown_hi[:].bitcast(F32), ALU.subtract).then_inc(bdown_rdy, 1)

            def elu1(q):
                dve.wait_ge(exp1_rdy, q + 1)
                nc.vector.tensor_scalar(exp1[:, pair(q), :], exp1[:, pair(q), :], 1.0, -1.0, ALU.min, ALU.add).then_inc(elu1_part, 1)
                dve.wait_ge(elu1_part, q + 1)
                nc.vector.tensor_tensor(exp1[:, pair(q), :], bank[:, 4 + q, :].rearrange("p (c n) -> p c n", c=2),
                                        exp1[:, pair(q), :], ALU.max).then_inc(elu1_rdy, 1)
                dve.wait_ge(elu1_rdy, q + 1)
                dve.wait_ge(gates_rdy, 1)
                nc.vector.scalar_tensor_tensor(out=xa[:, pair(q), :], in0=exp1[:, pair(q), :], scalar=gates[:, 0:1],
                                               in1=x_sb[:, pair(q), :], op0=ALU.mult, op1=ALU.add).then_inc(xa_rdy, 1)
                dve.wait_ge(xa_rdy, q + 1)

            def check_peaks():
                dve.wait_ge(check_ld, 48)
                dve.wait_ge(peaks_part, 1)
                nc.vector.tensor_reduce(peaks[:, 0:1], ctx_sb[:], AX.XY, ALU.max, apply_absolute_value=True).then_inc(peaks_part, 1)
                nc.vector.tensor_reduce(bound[:, 0:2], w0t_sb[:], AX.X, ALU.add, apply_absolute_value=True).then_inc(peaks_part, 1)
                nc.vector.tensor_reduce(bound[:, 2:4], w1t_sb[:], AX.X, ALU.add, apply_absolute_value=True).then_inc(peaks_part, 1)
                nc.vector.tensor_reduce(peaks[0:H, 3:7], a_sb[:], AX.X, ALU.add, apply_absolute_value=True).then_inc(peaks_part, 1)
                nc.vector.tensor_reduce(peaks[:, 7:8], b0_sb[:], AX.X, ALU.max, apply_absolute_value=True).then_inc(peaks_part, 1)
                dve.wait_ge(peaks_part, 6)
                nc.vector.tensor_reduce(peaks[:, 1:3], bound[:, 0:4].rearrange("p (k c) -> p k c", c=2), AX.X, ALU.max
                                        ).then_inc(peaks_rdy, 1)

            def check_rows():
                for t in range(NT):
                    nc.vector.bn_stats(xstat[:, t, :], x_sb[:, t, :]).then_inc(xstat_rdy, 1)
                for t in range(NT):
                    dve.wait_ge(xstat_rdy, max(NT, t + 1))
                    nc.vector.bn_aggr(xmv[:, t, :], xstat[:, t, :]).then_inc(xstat_rdy, 1)

            def check_flag():
                dve.wait_ge(good_rdy, 1)
                nc.vector.tensor_reduce(flag_f[:], good_all[:], AX.X, ALU.min).then_inc(flag_step, 1)
                dve.wait_ge(flag_step, 1)
                nc.vector.tensor_scalar(flag_f[:], flag_f[:], float(P), None, ALU.is_lt).then_inc(flag_step, 1)
                dve.wait_ge(flag_step, 2)
                nc.vector.tensor_copy(flag[:], flag_f[:]).then_inc(flag_rdy, 1)

            for q in range(HALVES):
                elu1(q)
            dve_experts(dve, 0, elu1, check_peaks, check_rows, check_flag)

            def general():
                nc.vector.memset(nmax[:], 0.0).then_inc(g_xa, 1)
                with dve.Fori(0, B) as b:
                    def link(ins, base):
                        ins.then_inc(g_vec, 1)
                        dve.wait_ge(g_vec, base)

                    g0 = b * VEC_GRAPH
                    link(nc.vector.tensor_scalar(gve[:], xmv[:, bass.ds(b * C, C), 1], EPS, None, ALU.add), g0 + 1)
                    dve.wait_ge(g_sqrt, b + 1)
                    link(nc.vector.reciprocal(grstd[:], grstd[:]), g0 + 2)
                    for c in range(C):
                        link(nc.vector.tensor_scalar(mask[:, c, :], x_sb[:, bass.ds(b * C + c, 1), :].rearrange("p a n -> p (a n)"), xmv[:, bass.ds(b * C + c, 1), 0], grstd[:, c:c + 1],
                                                     ALU.subtract, ALU.mult), g0 + (3 + c))
                    link(nc.vector.tensor_scalar(mask, mask, -1.0, 1.0, ALU.mult, ALU.add), g0 + 5)
                    link(nc.vector.tensor_scalar(mask, mask, -MASK, None, ALU.mult), g0 + 6)
                    dve.wait_ge(g_bc_ld, 96)
                    for l in range(2):
                        l0 = g0 + (6 + l * VEC_LAYER)
                        dve.wait_ge(g_feat, b * 2 + (l + 1))
                        for k in range(2):
                            link(nc.vector.tensor_tensor(fprod, feat,
                                                         a_bc[2 * l + k].broadcast_to([P, C, H * FO]),
                                                         ALU.mult), l0 + (2 * k + 1))
                            nc.vector.tensor_reduce(att[:, k, :, :], fprod.rearrange("p c (h o) -> p c h o", h=H),
                                                    AX.X, ALU.add).then_inc(g_vec, 1)
                            if k == 0:
                                dve.wait_ge(g_vec, l0 + 2)
                        with dve.Fori(0, H) as h:
                            turn = b * (2 * H) + h + (l * H + 1)
                            h0 = l0 + h * VEC_HEAD + 4
                            dve.wait_ge(g_vec, l0 + 4)
                            for j in range(C):
                                ins = nc.vector.tensor_scalar(diag[:, j, :], ident[:], att[:, 1, j, bass.ds(h, 1)], None, ALU.mult)
                            ins.then_inc(g_diag, 1)
                            dve.wait_ge(g_row_mm, turn)
                            for i in range(C):
                                link(nc.vector.tensor_scalar(sc[:, i, :], bank[:, 1, 0:N], att[:, 0, i, bass.ds(h, 1)],
                                                             None, ALU.add), h0 + (1 + i))
                            link(nc.vector.scalar_tensor_tensor(out=sc2, in0=sc, scalar=LRELU, in1=sc,
                                                                op0=ALU.mult, op1=ALU.max), h0 + 3)
                            link(nc.vector.tensor_tensor(sc2, sc2, mask, ALU.add), h0 + 4)
                            nc.vector.tensor_reduce(nmax[:], sc2, AX.X, ALU.max, negate=True).then_inc(g_max, 1)
                            dve.wait_ge(g_exp, turn * 2)
                            link(nc.vector.reciprocal(rsum[:], psum_p[:]), h0 + 5)
                            for i in range(C):
                                nc.vector.tensor_scalar(alpha[:, i, :], pr[:, i, :], rsum[:, i:i + 1], None,
                                                        ALU.mult).then_inc(g_alpha, 1)
                        lt = l0 + 4 + H * VEC_HEAD
                        dve.wait_ge(g_out_mm, b * (2 * H) + (l + 1) * H)
                        nc.vector.tensor_tensor(gz, bank[:, 3, :].rearrange("p (c n) -> p c n", c=C),
                                                b_bc[:, l:l + 1, :].broadcast_to([P, C, H * FO]), ALU.add).then_inc(g_z, 1)
                        dve.wait_ge(g_zexp, b * 2 + (l + 1))
                        link(nc.vector.tensor_scalar(gu, gexp, 1.0, -1.0, ALU.min, ALU.add), lt + 1)
                        nc.vector.tensor_tensor(gh, gz, gu, ALU.max).then_inc(g_h, 1)
                        dve.wait_ge(g_h, b * 2 + (l + 1))
                    nc.vector.scalar_tensor_tensor(out=xa[:, bass.ds(b * C, C), :], in0=gh, scalar=gates[:, 0:1], in1=x_sb[:, bass.ds(b * C, C), :],
                                                   op0=ALU.mult, op1=ALU.add).then_inc(g_xa, 1)
                    dve.wait_ge(g_xa, b + 2)
                dve_experts(dve, 1, None, None, None, None)

            on_general(dve, general)



_OUT = ("out", (B, N, D))


def kernel(x, ctx_512, g_xattn, g_ffn, L0_xattn_W0, L0_xattn_a_self0, L0_xattn_a_neigh0, L0_xattn_b0, L0_xattn_W1,
           L0_xattn_a_self1, L0_xattn_a_neigh1, L0_xattn_b1, L0_ffn_Wg1, L0_ffn_Wg2, L0_ffn_Wup, L0_ffn_bup,
           L0_ffn_Wdown, L0_ffn_bdown):
    import concourse.bacc as bacc
    from concourse.bass_utils import run_bass_kernel_spmd

    def a(v):
        return np.asarray(v)

    ctx = a(ctx_512)
    w0 = a(L0_xattn_W0).transpose(1, 0, 2).reshape(FIN, H * FO)
    w1 = a(L0_xattn_W1).transpose(1, 0, 2).reshape(H * FO, H * FO)
    arrays = {
        "x": a(x),
        "ctx": ctx,
        "ctx_t": ctx.reshape(T, FIN).T,
        "g2": np.concatenate([a(g_xattn), a(g_ffn)]).reshape(1, 2),
        "w0": w0,
        "w0_t": w0.T,
        "b0_c": a(L0_xattn_b0).reshape(C, P).T,
        "b0_r": a(L0_xattn_b0).reshape(1, H * FO),
        "w1": w1,
        "w1_t": w1.T,
        "b1_r": a(L0_xattn_b1).reshape(1, H * FO),
        "avec": np.stack([a(L0_xattn_a_self0), a(L0_xattn_a_neigh0), a(L0_xattn_a_self1), a(L0_xattn_a_neigh1)]),
        "wg1": a(L0_ffn_Wg1).T,
        "wg2_r": a(L0_ffn_Wg2).reshape(1, E * E),
        "wup": a(L0_ffn_Wup).reshape(E * HE, D).T,
        "bup_c": a(L0_ffn_bup).T,
        "wdown": a(L0_ffn_Wdown).transpose(0, 2, 1),
        "bdown": a(L0_ffn_bdown),
    }
    nc = bacc.Bacc("TRN2", target_bir_lowering=False, num_devices=1)
    feed, args = {}, []
    for name, v in arrays.items():
        feed[f"in_{name}"] = np.ascontiguousarray(v)
        args.append(nc.dram_tensor(f"in_{name}", v.shape, mybir.dt.from_np(v.dtype), kind="ExternalInput").ap())
    args.append(nc.dram_tensor(_OUT[0], _OUT[1], F32, kind="ExternalOutput").ap())
    build(nc, *args)
    r = run_bass_kernel_spmd(nc, [feed], core_ids=[0])
    return r.results[0][_OUT[0]]
```

```python
from contextlib import ExitStack

import numpy as np

import concourse.bass as bass
from concourse import mybir

ALU = mybir.AluOpType
ACT = mybir.ActivationFunctionType
AX = mybir.AxisListType
F32 = mybir.dt.float32
F32R = mybir.dt.float32r
BF16 = mybir.dt.bfloat16
I32 = mybir.dt.int32
U32 = mybir.dt.uint32

P = 128
B, N, D = 4, 256, 256
FIN = 64
H, FO = 8, 32
E, HE = 8, 128
T = B * N
NT = T // P
C = N // P
STEPS = B * E
PICK_LAG = 8
DOWN_LAG = PICK_LAG + 3
SILU_SLOTS = PICK_LAG + 2
HID_SLOTS = 4
SCORE_PLACE = (7, 6, 6, 6)
WQ = 4
EQ = E // WQ
EPS = 1e-5
MASK = 1e10
LRELU = 0.2

PK_W0, PK_B0, PK_GATE, PK_BUP, PK_WG1, PK_WG2 = 0, 256, 258, 260, 268, 284
PK = PK_WG2 + E * E


def build(nc, x, ctx_in, ctx_t, small, w1, bias_2, b0_r, b1_r, wup, wdown, bdown_2, check_w, avec, out):
    with ExitStack() as stack:
        def sb(name, shape, dt=F32):
            return stack.enter_context(nc.sbuf_tensor(name, shape, dt))

        def sem(name):
            return stack.enter_context(nc.semaphore(name))

        x_sb = sb("x_sb", [P, NT, D])
        ctx_sb = sb("ctx_sb", [P, NT, FIN])
        small_sb = sb("small_sb", [P, PK])
        w0_sb = small_sb[:, PK_W0:PK_B0]
        b0_sb = small_sb[:, PK_B0:PK_GATE]
        bup_sb = small_sb[:, PK_BUP:PK_WG1]
        wg1_sb = small_sb[:, PK_WG1:PK_WG2].rearrange("p (c e) -> p c e", c=C)
        wg2_sb = small_sb[:, PK_WG2:PK].rearrange("p (e k) -> p e k", e=E)
        gates = sb("gates", [P, 2])
        w1_sb = sb("w1_sb", [P, C, H * FO])
        bias_sb = sb("bias_sb", [64, 2, H * FO])
        wup_sb = sb("wup_sb", [P, C, E * HE])
        wdown_sb = sb("wdown_sb", [P, E, D])
        bdown_sb = sb("bdown_sb", [2 * E, D])
        check_sb = sb("check_sb", [P, C * (FIN + H * FO)])
        a_sb = sb("a_sb", [H, 4, FO])
        w0_hi, w0_lo = sb("w0_hi", [P, H * FO], F32R), sb("w0_lo", [P, H * FO], F32R)
        w1_hi, w1_lo = sb("w1_hi", [P, C, H * FO], F32R), sb("w1_lo", [P, C, H * FO], F32R)
        wup_hi, wup_lo = sb("wup_hi", [P, C, E * HE], F32R), sb("wup_lo", [P, C, E * HE], F32R)
        wdown_hi, wdown_lo = sb("wdown_hi", [P, E, D], F32R), sb("wdown_lo", [P, E, D], F32R)
        bdown_hi, bdown_lo = sb("bdown_hi", [2 * E, D], F32R), sb("bdown_lo", [2 * E, D], F32R)
        wg1_parts = sb("wg1_parts", [P, C, 2 * E], F32R)
        bias_parts = sb("bias_parts", [64, 2, H * FO], F32R)
        ctx_parts = sb("ctx_parts", [P, NT, 2 * FIN], F32R)
        ident = sb("ident", [P, P])
        ident_bf = sb("ident_bf", [P, P], BF16)
        ones = sb("ones", [P, P])
        ones_r = sb("ones_r", [64, N], F32R)
        pick = sb("pick", [2 * E, E, P], F32R)
        expert_no = sb("expert_no", [P, E])
        powers = sb("powers", [P, 2 * NT])
        top = sb("top", [P, NT, 8])
        onehot = sb("onehot", [P, NT, N], BF16)
        onehot_t = sb("onehot_t", [P, B, C, N], F32R)
        once = sb("once", [P, B, C, 2 * FIN], F32R)
        twice = sb("twice", [P, B, N], F32R)
        elu_exp = sb("elu_exp", [P, B, C, N])
        h1 = sb("h1", [P, B, C, N])
        h1_hi, h1_lo = sb("h1_hi", [P, B, C, N], F32R), sb("h1_lo", [P, B, C, N], F32R)
        xa = sb("xa", [P, NT, D])
        peaks = sb("peaks", [P, 8])
        peaks_all = sb("peaks_all", [P, 8])
        colsum = sb("colsum", [P, 2 * C])
        bound = sb("bound", [P, 8])
        xsq = sb("xsq", [P, NT])
        rms = sb("rms", [P, NT])
        lead = sb("lead", [P, NT])
        need = sb("need", [P, NT])
        size = sb("size", [P, NT])
        good = sb("good", [P, NT])
        good_all = sb("good_all", [P, NT])
        flag_f = sb("flag_f", [P, 1])
        flag = sb("flag", [P, 1], I32)
        stat = sb("stat", [P, NT, 6])
        mv = sb("mv", [P, NT, 2])
        veps = sb("veps", [P, NT])
        rstd = sb("rstd", [P, NT])
        xn = sb("xn", [P, NT, D])
        xt_hi, xt_lo = sb("xt_hi", [P, B, C, N], F32R), sb("xt_lo", [P, B, C, N], F32R)
        gate_in = sb("gate_in", [P, NT, E])
        gate_h = sb("gate_h", [P, NT, E])
        gate_prod = sb("gate_prod", [P, C, E, E])
        logits = sb("logits", [P, NT, E])
        ltop = sb("ltop", [P, NT, 8])
        lidx = sb("lidx", [P, NT, 8], U32)
        lidx_f = sb("lidx_f", [P, NT, 8])
        ldiff = sb("ldiff", [P, NT])
        lth = sb("lth", [P, NT])
        prob = sb("prob", [P, 2, NT])
        hit = sb("hit", [P, 2, NT, E])
        score = sb("score", [P, NT, E])
        score_hi = sb("score_hi", [P, NT, E], F32R)
        score_parts = sb("score_parts", [P, NT, 2 * E])
        score_t = sb("score_t", [2 * E, B, N], F32R)
        act_more = sb("act_more", [P, SILU_SLOTS - B * C, N])
        hid = sb("hid", [P, 2, N])
        hid_hi, hid_lo = sb("hid_hi", [P, HID_SLOTS, N], F32R), sb("hid_lo", [P, HID_SLOTS, N], F32R)
        out_sb = sb("out_sb", [P, NT, D])
        pick_f = out_sb[0:2 * E, 0:E * P // D, :].rearrange("k a (b n) -> k (a b) n", n=P)

        def slots(t):
            flat = t.rearrange("p b c n -> p (b c n)") if len(t.shape) == 4 else t.rearrange("p a b -> p (a b)")
            return [flat[:, k * C * N:(k + 1) * C * N].rearrange("p (c n) -> p c n", c=C) for k in range(4)]

        gz, gexp, pr, alpha_t = slots(elu_exp[:])
        sc, sc2, alpha, gh = slots(h1[:])
        feat, fprod, gh_t, spare_slot = slots(out_sb[:])
        mask, a01_bc, a23_bc, b_bc = slots(xn[:])
        gneg = fprod
        diag = spare_slot[:, 0, :].rearrange("p (c n) -> p c n", c=C)
        ctxt_b = spare_slot[0:FIN, 1, :]
        a_bc = [a01_bc[:, 0:1, :], a01_bc[:, 1:2, :], a23_bc[:, 0:1, :], a23_bc[:, 1:2, :]]
        xstat = sb("xstat", [P, NT, 6])
        xmv = sb("xmv", [P, NT, 2])
        gve = sb("gve", [P, C])
        grstd = sb("grstd", [P, C])
        att = sb("att", [P, 2, C, H])
        nmax = sb("nmax", [P, C])
        psum_p = sb("psum_p", [P, C])
        rsum = sb("rsum", [P, C])

        bank = stack.enter_context(nc.psum_tensor("bank", [P, 8, 512], F32))
        TURN, ONCE, TWICE, FEAT0, FEAT1 = (2, 0, 2, 0), 4, 5, (6, 7, 6, 7), (1, 3, 6, 7)
        XT, ROUTE, UP, PICK, DOWN = 0, 2, (4, 5), (1, 3), (6, 7)

        x_in = [sem(f"x_in{b}") for b in range(B)]
        ctx_ld, small_ld, w1_ld, bias_ld, wup_ld, wdown_ld, bdown_ld, check_ld = (
            sem(n) for n in ("ctx_ld", "small_ld", "w1_ld", "bias_ld", "wup_ld", "wdown_ld", "bdown_ld", "check_ld"))
        raw_zero, ident_bf_rdy, ident_rdy, pick_raw, pick_rdy, consts_rdy, ones_r_rdy, gates_rdy, bias_zero = (
            sem(n) for n in ("raw_zero", "ident_bf_rdy", "ident_rdy", "pick_raw", "pick_rdy", "consts_rdy", "ones_r_rdy",
                             "gates_rdy", "bias_zero"))
        ctx_hi_rdy, ctx_lo_rdy, w0_hi_rdy, w0_lo_rdy, w1_hi_rdy, w1_lo_rdy, wup_hi_rdy, wup_hi2_rdy, wup_lo_rdy = (
            sem(n) for n in ("ctx_hi_rdy", "ctx_lo_rdy", "w0_hi_rdy", "w0_lo_rdy", "w1_hi_rdy", "w1_lo_rdy", "wup_hi_rdy",
                             "wup_hi2_rdy", "wup_lo_rdy"))
        wdown_hi_rdy, wdown_lo_rdy, bdown_hi_rdy, bdown_lo_rdy, wg1_hi_rdy, wg1_lo_rdy, bias_hi_rdy, bias_rdy = (
            sem(n) for n in ("wdown_hi_rdy", "wdown_lo_rdy", "bdown_hi_rdy", "bdown_lo_rdy", "wg1_hi_rdy", "wg1_lo_rdy",
                             "bias_hi_rdy", "bias_rdy"))
        top_rdy, onehot_rdy, onehot2_rdy, turn_mm, onehot_t_rdy, onehot_t2_rdy, once_mm, once_rdy, twice_mm, twice_rdy = (
            sem(n) for n in ("top_rdy", "onehot_rdy", "onehot2_rdy", "turn_mm", "onehot_t_rdy", "onehot_t2_rdy", "once_mm", "once_rdy", "twice_mm",
                             "twice_rdy"))
        feat0_mm, neg0_rdy, exp0_rdy, h1_rdy, h1_hi_rdy, h1_hi2_rdy, h1_lo_rdy = (
            sem(n) for n in ("feat0_mm", "neg0_rdy", "exp0_rdy", "h1_rdy", "h1_hi_rdy", "h1_hi2_rdy", "h1_lo_rdy"))
        feat1_mm, neg1_rdy, exp1_rdy, elu1_rdy, xa_rdy = (
            sem(n) for n in ("feat1_mm", "neg1_rdy", "exp1_rdy", "elu1_rdy", "xa_rdy"))
        peaks_part, peaks_rdy, peaks_all_rdy, check_step, xsq_rdy, flag_step, good_rdy, flag_rdy = (
            sem(n) for n in ("peaks_part", "peaks_rdy", "peaks_all_rdy", "check_step", "xsq_rdy", "flag_step", "good_rdy",
                             "flag_rdy"))
        stat_rdy, mv_rdy, veps_rdy, rstd_rdy, xn_rdy, xt_mm, xt_hi_rdy, xt_lo_rdy = (
            sem(n) for n in ("stat_rdy", "mv_rdy", "veps_rdy", "rstd_rdy", "xn_rdy", "xt_mm", "xt_hi_rdy", "xt_lo_rdy"))
        gate_mm, gate_in_rdy, gate_h_rdy, logit_step, ldiff_rdy, lidx_rdy, lth_rdy, score_step, score_rdy, score_mm, score_t_rdy = (
            sem(n) for n in ("gate_mm", "gate_in_rdy", "gate_h_rdy", "logit_step", "ldiff_rdy", "lidx_rdy", "lth_rdy",
                             "score_step", "score_rdy", "score_mm", "score_t_rdy"))
        up_mm, pick_mm, silu_rdy, hid_rdy, hid_hi_rdy, hid_lo_rdy, down_mm, out_rdy, stored = (
            sem(n) for n in ("up_mm", "pick_mm", "silu_rdy", "hid_rdy", "hid_hi_rdy", "hid_lo_rdy", "down_mm", "out_rdy",
                             "stored"))
        g_bc_ld, g_graph_ld, g_stat, g_mv, g_vec, g_sqrt, g_feat_mm, g_feat, g_diag, g_row_mm, g_max, g_exp = (
            sem(n) for n in ("g_bc_ld", "g_graph_ld", "g_stat", "g_mv", "g_vec", "g_sqrt", "g_feat_mm", "g_feat", "g_diag",
                             "g_row_mm", "g_max", "g_exp"))
        g_alpha, g_alpha_mm, g_alpha_t, g_out_mm, g_z, g_neg, g_zexp, g_h, g_h_mm, g_h_t, g_xa = (
            sem(n) for n in ("g_alpha", "g_alpha_mm", "g_alpha_t", "g_out_mm", "g_z", "g_neg", "g_zexp", "g_h", "g_h_mm",
                             "g_h_t", "g_xa"))

        block = stack.enter_context(nc.Block())

        VEC_HEAD = 5
        VEC_LAYER = 4 + H * VEC_HEAD
        VEC_GRAPH = 6 + 2 * VEC_LAYER
        LOGIT_STEPS = 2 + C
        SCORE_STEPS = 9

        def pair(b):
            return slice(C * b, C * b + C)

        def act_out(n):
            k = n % SILU_SLOTS
            return elu_exp[:, k // C, k % C, :] if k < B * C else act_more[:, k - B * C, :]

        def turned_bank(b):
            return bank[:, TURN[b], 0:N].bitcast(BF16).rearrange("p (c n) -> p c n", c=C)

        def both(k):
            return bank[:, k, :].rearrange("p (c n) -> p c n", c=C)

        def quarter(q):
            return slice(q * EQ * HE, (q + 1) * EQ * HE), slice(q * EQ, (q + 1) * EQ)

        def on_general(eng, body):
            eng.wait_ge(flag_rdy, 1)
            v = eng.value_load(flag[0:1, 0:1])
            with eng.If(v != 0):
                body()
            with eng.Else():
                eng.wait_ge(flag_rdy, 1)
            eng.wait_ge(flag_rdy, 1)

        @block.sync
        def _(sp):
            def load_x(b):
                sp.dma_start(x_sb[:, pair(b), :], x[b].rearrange("(c p) d -> p c d", p=P)).then_inc(x_in[b], 16)

            load_x(0)
            load_x(1)
            sp.dma_start(small_sb[:], small).then_inc(small_ld, 16)
            sp.wait_ge(bias_zero, 1)
            sp.dma_start(bias_sb[0:33:32, :, :], bias_2).then_inc(bias_ld, 16)
            load_x(2)
            load_x(3)
            sp.dma_start(w1_sb[:], w1).then_inc(w1_ld, 16)
            sp.dma_start(wup_sb[:], wup).then_inc(wup_ld, 16)
            sp.dma_start(wdown_sb[:], wdown).then_inc(wdown_ld, 16)
            sp.dma_start(bdown_sb[:], bdown_2).then_inc(bdown_ld, 16)
            sp.dma_start(check_sb[:], check_w).then_inc(check_ld, 16)
            sp.dma_start(a_sb[:], avec.rearrange("k h o -> h k o")).then_inc(check_ld, 16)

            def store(run):
                for b in range(B - 1):
                    sp.wait_ge(out_rdy, NT * run + C * (b + 1))
                    sp.dma_start(out[b].rearrange("(c p) d -> p c d", p=P), out_sb[:, pair(b), :]).then_inc(stored, 16)
                for t in range(C):
                    sp.wait_ge(out_rdy, NT * (run + 1) - C + t + 1)
                    sp.dma_start(out[B - 1, t * P:(t + 1) * P, :], out_sb[:, NT - C + t, :]).then_inc(stored, 16)
                sp.wait_ge(stored, 16 * (B - 1 + C) * (run + 1))

            store(0)

            def general():
                sp.dma_start(b_bc[:, 0, :], b0_r.broadcast_to([P, H * FO])).then_inc(g_bc_ld, 16)
                sp.dma_start(b_bc[:, 1, :], b1_r.broadcast_to([P, H * FO])).then_inc(g_bc_ld, 16)
                for k in range(4):
                    sp.dma_start(a_bc[k][:, 0, :], avec[k].rearrange("h o -> (h o)").rearrange("(a n) -> a n", a=1)
                                 .broadcast_to([P, H * FO])).then_inc(g_bc_ld, 16)
                with sp.Fori(0, B) as b:
                    sp.wait_ge(g_xa, b + 1)
                    sp.dma_start(ctxt_b, ctx_t[:, bass.ds(b * N, N)]).then_inc(g_graph_ld, 16)
                store(1)

            on_general(sp, general)

        def row_power(pool, run, b):
            nb = run * B + b
            pool.wait_ge(mv_rdy, (nb + 1) * C)
            nc.gpsimd.tensor_scalar(veps[:, pair(b)], mv[:, pair(b), 1], EPS, None, ALU.add).then_inc(veps_rdy, 1)
            pool.wait_ge(veps_rdy, nb + 1)
            nc.gpsimd.tensor_tensor(rstd[:, pair(b)], veps[:, pair(b)], powers[:, 0:C], ALU.pow).then_inc(rstd_rdy, 1)

        def scores(pool, run, b):
            nb = run * B + b
            r = pair(b)
            done = [nb * SCORE_STEPS]

            def link(ins, chained=True):
                done[0] += 1
                ins.then_inc(score_step, 1)
                if chained:
                    pool.wait_ge(score_step, done[0])

            pool.wait_ge(lidx_rdy, C * (nb + 1))
            link(nc.gpsimd.tensor_copy(lidx_f[:, r, 0:2], lidx[:, r, 0:2]))
            pool.wait_ge(lth_rdy, nb + 1)
            link(nc.gpsimd.tensor_scalar(prob[:, 0, r], lth[:, r], 0.5, 0.5, ALU.mult, ALU.add), False)
            link(nc.gpsimd.tensor_scalar(prob[:, 1, r], lth[:, r], -0.5, 0.5, ALU.mult, ALU.add))
            for k in range(2):
                for t in range(C * b, C * b + C):
                    link(nc.gpsimd.tensor_scalar(hit[:, k, t, :], expert_no[:], lidx_f[:, t, k:k + 1], prob[:, k, t:t + 1],
                                                 ALU.is_equal, ALU.mult), k == 1 and t == C * b + C - 1)
            link(nc.gpsimd.tensor_tensor(score[:, r, :], hit[:, 0, r, :], hit[:, 1, r, :], ALU.add))
            link(nc.gpsimd.tensor_copy(score_hi[:, r, :], score[:, r, :]))
            if run >= 1:
                pool.wait_ge(score_mm, run * B)
            nc.gpsimd.tensor_copy(score_parts[:, r, 0:E], score_hi[:, r, :].bitcast(F32)).then_inc(score_rdy, 1)
            nc.gpsimd.tensor_tensor(score_parts[:, r, E:2 * E], score[:, r, :], score_hi[:, r, :].bitcast(F32),
                                    ALU.subtract).then_inc(score_rdy, 1)
            assert done[0] == (nb + 1) * SCORE_STEPS

        @block.gpsimd
        def _(pool):
            nc.gpsimd.memset(ident_bf[:], 0.0).then_inc(raw_zero, 1)
            nc.gpsimd.memset(pick_f, 0.0).then_inc(raw_zero, 1)
            nc.gpsimd.memset(ident[:], 0.0).then_inc(raw_zero, 1)
            pool.wait_ge(raw_zero, 1)
            nc.gpsimd.affine_select(out=ident_bf[:], in_=ident_bf[:], compare_op=ALU.not_equal, fill=1.0, base=0,
                                    pattern=[[-1, P]], channel_multiplier=1).then_inc(ident_bf_rdy, 1)
            pool.wait_ge(raw_zero, 3)
            nc.gpsimd.affine_select(out=ident[:], in_=ident[:], compare_op=ALU.not_equal, fill=1.0, base=0,
                                    pattern=[[-1, P]], channel_multiplier=1).then_inc(ident_rdy, 1)
            nc.gpsimd.affine_select(out=pick_f, in_=pick_f, compare_op=ALU.not_equal, fill=1.0, base=0,
                                    pattern=[[-1, E], [0, P]], channel_multiplier=1).then_inc(pick_raw, 1)
            pool.wait_ge(pick_raw, 1)
            nc.gpsimd.affine_select(out=pick_f, in_=pick_f, compare_op=ALU.not_equal, fill=1.0, base=-E,
                                    pattern=[[-1, E], [0, P]], channel_multiplier=1).then_inc(pick_raw, 1)
            nc.gpsimd.iota(expert_no[:], pattern=[[1, E]], base=0, channel_multiplier=0,
                           allow_small_or_imprecise_dtypes=True).then_inc(consts_rdy, 1)
            nc.gpsimd.memset(ones[:], 1.0).then_inc(consts_rdy, 1)
            nc.gpsimd.memset(powers[:, 0:NT], -0.5).then_inc(consts_rdy, 1)
            nc.gpsimd.memset(powers[:, NT:2 * NT], 0.5).then_inc(consts_rdy, 1)
            pool.wait_ge(consts_rdy, 4)
            for t in range(2 * C, 3 * C):
                pool.wait_ge(top_rdy, t + 1)
                nc.gpsimd.tensor_scalar(onehot[:, t, :], x_sb[:, t, :], top[:, t, 0:1], None,
                                        ALU.is_equal).then_inc(onehot2_rdy, 1)
            pool.wait_ge(w1_hi_rdy, 1)
            nc.gpsimd.tensor_tensor(w1_lo[:], w1_sb[:], w1_hi[:].bitcast(F32), ALU.subtract).then_inc(w1_lo_rdy, 1)

            def wup_part(q):
                cols, _ = quarter(q)
                if q == 0:
                    pool.wait_ge(wup_hi_rdy, 1)
                else:
                    pool.wait_ge(wup_hi2_rdy, q)
                nc.gpsimd.tensor_tensor(wup_lo[:, :, cols], wup_sb[:, :, cols], wup_hi[:, :, cols].bitcast(F32),
                                        ALU.subtract).then_inc(wup_lo_rdy, 1)

            def wdown_part(q):
                _, es = quarter(q)
                pool.wait_ge(wdown_hi_rdy, q + 1)
                nc.gpsimd.tensor_tensor(wdown_lo[:, es, :], wdown_sb[:, es, :], wdown_hi[:, es, :].bitcast(F32),
                                        ALU.subtract).then_inc(wdown_lo_rdy, 1)

            wup_part(0)
            wup_part(1)
            row_power(pool, 0, 0)
            wup_part(2)
            wup_part(3)
            row_power(pool, 0, 1)
            scores(pool, 0, 0)
            row_power(pool, 0, 2)
            wdown_part(0)
            wdown_part(1)
            wdown_part(2)
            wdown_part(3)
            scores(pool, 0, 1)
            row_power(pool, 0, 3)

            done = [0]

            def link(ins):
                done[0] += 1
                ins.then_inc(check_step, 1)
                pool.wait_ge(check_step, done[0])

            def tt(o, a, b, op):
                link(nc.gpsimd.tensor_tensor(o, a, b, op))

            def ts(o, a, *rest):
                link(nc.gpsimd.tensor_scalar(o, a, *rest))

            def check_bound():
                pool.wait_ge(peaks_rdy, 1)
                nc.gpsimd.partition_all_reduce(peaks_all[:], peaks[:], P, bass.bass_isa.ReduceOp.max).then_inc(peaks_all_rdy, 1)
                pool.wait_ge(peaks_all_rdy, 1)
                cmax, c0, c1, as0, an0, as1, an1, b0max = (peaks_all[:, k:k + 1] for k in range(8))
                feat0, a0, a1, l1, l0, total, margin = (bound[:, k:k + 1] for k in range(7))
                tt(feat0, cmax, c0, ALU.mult)
                tt(a0, as0, an0, ALU.add)
                tt(a1, as1, an1, ALU.add)
                tt(l1, feat0, b0max, ALU.add)
                ts(l1, l1, 1.0, None, ALU.max)
                tt(l1, l1, c1, ALU.mult)
                tt(l1, l1, a1, ALU.mult)
                tt(l0, feat0, a0, ALU.mult)
                tt(total, l0, l1, ALU.add)
                ts(margin, total, 3.0 / MASK, 200.0 / MASK + 2e-6, ALU.mult, ALU.add)

            def check_rows():
                pool.wait_ge(xsq_rdy, NT)
                ts(rms[:], xsq[:], 1.0 / D, EPS, ALU.mult, ALU.add)
                tt(rms[:], rms[:], powers[:, NT:2 * NT], ALU.pow)
                tt(lead[:], top[:, :, 0], top[:, :, 1], ALU.subtract)
                ts(size[:], top[:, :, 0], -1.0, 0.0, ALU.mult, ALU.max)
                ts(good[:], top[:, :, 0], 0.0, None, ALU.max)
                tt(size[:], size[:], good[:], ALU.add)
                tt(size[:], size[:], rms[:], ALU.add)
                ts(size[:], size[:], 2e-6, None, ALU.mult)
                ts(need[:], rms[:], bound[:, 6:7], None, ALU.mult)
                tt(need[:], need[:], size[:], ALU.add)
                tt(lead[:], lead[:], need[:], ALU.subtract)
                ts(good[:], lead[:], 0.0, None, ALU.is_gt)
                nc.gpsimd.partition_all_reduce(good_all[:], good[:], P, bass.bass_isa.ReduceOp.add).then_inc(good_rdy, 1)

            check_bound()
            scores(pool, 0, 2)
            check_rows()
            scores(pool, 0, 3)

            def general():
                for b in range(B):
                    row_power(pool, 1, b)
                for b in range(B):
                    scores(pool, 1, b)

            on_general(pool, general)

        def act_xt(act, run, b):
            act.wait_ge(xt_mm, run * B + b + 1)
            nc.scalar.copy(xt_hi[:, b, :, :], both(XT)).then_inc(xt_hi_rdy, 1)

        def act_gate(act, run, b):
            act.wait_ge(gate_in_rdy, run * B + b + 1)
            nc.scalar.activation(gate_h[:, pair(b), :], gate_in[:, pair(b), :], ACT.Tanh).then_inc(gate_h_rdy, 1)

        def act_diff(act, run, b):
            act.wait_ge(ldiff_rdy, run * B + b + 1)
            nc.scalar.activation(lth[:, pair(b)], ldiff[:, pair(b)], ACT.Tanh, scale=0.5).then_inc(lth_rdy, 1)

        def act_silu(act, run, k):
            n = run * STEPS + k
            act.wait_ge(up_mm, n + 1)
            if n >= SILU_SLOTS:
                act.wait_ge(hid_rdy, n - SILU_SLOTS + 1)
            elif n % C == 0 and n < B * C:
                act.wait_ge(xa_rdy, n // C + 1)
            nc.scalar.activation(act_out(n), bank[:, UP[n % 2], 0:N], ACT.Silu,
                                 bias=bup_sb[:, k % E:k % E + 1]).then_inc(silu_rdy, 1)

        def act_hid(act, run, k):
            n = run * STEPS + k
            act.wait_ge(hid_rdy, n + 1)
            if n >= HID_SLOTS:
                act.wait_ge(down_mm, n - HID_SLOTS + 1)
            nc.scalar.copy(hid_hi[:, n % HID_SLOTS, :], hid[:, n % 2, :]).then_inc(hid_hi_rdy, 1)

        def act_experts(act, run):
            for i in range(STEPS + PICK_LAG):
                b, e = i // E, i % E
                if i < STEPS:
                    act_silu(act, run, i)
                    if b >= 1 and e == 2:
                        act_gate(act, run, b)
                    if e == (3 if b >= 1 else 1):
                        act_diff(act, run, b)
                if i >= PICK_LAG:
                    act_hid(act, run, i - PICK_LAG)
                if e == 4 and b + 1 < B:
                    act_xt(act, run, b + 1)
                if run == 0 and 12 <= i < 12 + NT:
                    t = i - 12
                    nc.scalar.activation(out_sq(t), x_sb[:, t, :], ACT.Square, accum_out=xsq[:, t:t + 1]).then_inc(xsq_rdy, 1)

        def out_sq(t):
            return h1[:, t // 2, t % 2, :]

        @block.scalar
        def _(act):
            act.dma_start(ctx_sb[:], ctx_in).then_inc(ctx_ld, 16)
            nc.scalar.preload_act_table(ACT.Exp)
            act.wait_ge(ctx_ld, 16)
            nc.scalar.copy(ctx_parts[:, :, 0:FIN], ctx_sb[:]).then_inc(ctx_hi_rdy, 1)

            def turned(b):
                act.wait_ge(turn_mm, b + 1)
                nc.scalar.copy(onehot_t[:, b, :, :], turned_bank(b)).then_inc(onehot_t_rdy, 1)

            def once_copy(b):
                act.wait_ge(once_mm, b + 1)
                nc.scalar.copy(once[:, b, :, :], bank[:, ONCE, 0:N].rearrange("p (c n) -> p c n", c=C)).then_inc(once_rdy, 1)

            def twice_copy(b):
                act.wait_ge(twice_mm, b + 1)
                nc.scalar.copy(twice[:, b, :], bank[:, TWICE, 0:N]).then_inc(twice_rdy, 1)

            def minus0(b):
                act.wait_ge(feat0_mm, b + 1)
                nc.scalar.activation(elu_exp[:, b, :, :], both(FEAT0[b]), ACT.Relu, scale=-1.0).then_inc(neg0_rdy, 1)

            def exp0(b):
                act.wait_ge(neg0_rdy, b + 1)
                nc.scalar.activation(elu_exp[:, b, :, :], elu_exp[:, b, :, :], ACT.Exp, scale=-1.0).then_inc(exp0_rdy, 1)

            def h1_part(b):
                act.wait_ge(h1_rdy, b + 1)
                nc.scalar.copy(h1_hi[:, b, :, :], h1[:, b, :, :]).then_inc(h1_hi2_rdy, 1)

            def minus1(b):
                act.wait_ge(feat1_mm, b + 1)
                nc.scalar.activation(elu_exp[:, b, :, :], both(FEAT1[b]), ACT.Relu, scale=-1.0).then_inc(neg1_rdy, 1)

            def exp1(b):
                act.wait_ge(neg1_rdy, b + 1)
                nc.scalar.activation(elu_exp[:, b, :, :], elu_exp[:, b, :, :], ACT.Exp, scale=-1.0).then_inc(exp1_rdy, 1)

            def wup_part(q):
                cols, _ = quarter(q)
                act.wait_ge(wup_ld, 16)
                nc.scalar.copy(wup_hi[:, :, cols], wup_sb[:, :, cols]).then_inc(wup_hi2_rdy, 1)

            turned(0)
            act.wait_ge(small_ld, 16)
            nc.scalar.copy(w0_hi[:], w0_sb).then_inc(w0_hi_rdy, 1)
            act.wait_ge(bias_ld, 16)
            nc.scalar.copy(bias_parts[:], bias_sb[:]).then_inc(bias_hi_rdy, 1)
            once_copy(0)
            twice_copy(0)
            turned(1)
            once_copy(1)
            nc.scalar.activation(gates[:], small_sb[:, PK_GATE:PK_BUP], ACT.Tanh).then_inc(gates_rdy, 1)
            minus0(0)
            exp0(0)
            twice_copy(1)
            wup_part(1)
            once_copy(2)
            minus0(1)
            twice_copy(2)
            exp0(1)
            wup_part(2)
            minus1(0)
            once_copy(3)
            exp1(0)
            minus0(2)
            twice_copy(3)
            exp0(2)
            minus0(3)
            h1_part(2)
            exp0(3)
            minus1(1)
            exp1(1)
            h1_part(3)
            minus1(2)
            act_xt(act, 0, 0)
            exp1(2)
            wup_part(3)
            minus1(3)
            exp1(3)
            act_gate(act, 0, 0)

            act_experts(act, 0)

            def general():
                with act.Fori(0, B) as b:
                    act.wait_ge(g_vec, b * VEC_GRAPH + 1)
                    nc.scalar.activation(grstd[:], gve[:], ACT.Sqrt).then_inc(g_sqrt, 1)
                    for l in range(2):
                        act.wait_ge(g_feat_mm, b * 2 + (l + 1))
                        nc.scalar.copy(feat, bank[:, 0, :]).then_inc(g_feat, 1)
                        with act.Fori(0, H) as h:
                            turn = b * (2 * H) + h + (l * H + 1)
                            act.wait_ge(g_max, turn)
                            for c in range(C):
                                nc.scalar.activation(pr[:, c, :], sc2[:, c, :], ACT.Exp, bias=nmax[:, c:c + 1],
                                                     accum_out=psum_p[:, c:c + 1]).then_inc(g_exp, 1)
                            act.wait_ge(g_alpha_mm, turn)
                            nc.scalar.copy(alpha_t, bank[:, 2, :]).then_inc(g_alpha_t, 1)
                        act.wait_ge(g_z, b * 2 + (l + 1))
                        nc.scalar.activation(gneg, gz, ACT.Relu, scale=-1.0).then_inc(g_neg, 1)
                        act.wait_ge(g_neg, b * 2 + (l + 1))
                        nc.scalar.activation(gexp, gneg, ACT.Exp, scale=-1.0).then_inc(g_zexp, 1)
                        if l == 0:
                            act.wait_ge(g_h_mm, b + 1)
                            nc.scalar.copy(gh_t, bank[:, 4, :]).then_inc(g_h_t, 1)

                act_xt(act, 1, 0)
                act_gate(act, 1, 0)
                act_experts(act, 1)

            on_general(act, general)

        def pe_xt(pe, run, b):
            nb = run * B + b
            if nb == 0:
                pe.wait_ge(ident_rdy, 1)
            else:
                pe.wait_ge(xt_lo_rdy, nb)
            pe.wait_ge(xn_rdy, C * (nb + 1))
            for c in range(C):
                for t in range(C):
                    mm = nc.tensor.transpose(both(XT)[:, c, t * P:(t + 1) * P], xn[:, C * b + t, c * P:(c + 1) * P], ident[:])
            mm.then_inc(xt_mm, 1)

        def pe_gate(pe, run, b):
            nb = run * B + b
            if nb == 0:
                pe.wait_ge(wg1_lo_rdy, 1)
            else:
                pe.wait_ge(score_t_rdy, nb)
            pe.wait_ge(xt_lo_rdy, nb + 1)
            for t in range(C):
                dst = bank[:, ROUTE, t * 2 * E:(t + 1) * 2 * E]
                for c in range(C):
                    nc.tensor.matmul(dst, xt_hi[:, b, c, t * P:(t + 1) * P], wg1_parts[:, c, :], start=(c == 0), stop=False)
                    mm = nc.tensor.matmul(dst, xt_lo[:, b, c, t * P:(t + 1) * P], wg1_parts[:, c, :],
                                          start=False, stop=(c == C - 1))
            mm.then_inc(gate_mm, 1)

        def pe_score(pe, run, b):
            pe.wait_ge(score_rdy, 2 * (run * B + b + 1))
            for t in range(C):
                mm = nc.tensor.transpose(bank[0:2 * E, ROUTE, t * P:(t + 1) * P], score_parts[:, C * b + t, :], ident[:])
            mm.then_inc(score_mm, 1)

        def pe_up(pe, run, k):
            n = run * STEPS + k
            b, e = k // E, k % E
            cols = slice(e * HE, (e + 1) * HE)
            if n >= 2:
                pe.wait_ge(silu_rdy, n - 1)
            if n < E and n % EQ == 0:
                pe.wait_ge(wup_lo_rdy, n // EQ + 1)
            if e == 0:
                pe.wait_ge(xt_lo_rdy, run * B + b + 1)
            dst = bank[:, UP[n % 2], 0:N]
            for c in range(C):
                nc.tensor.matmul(dst, wup_hi[:, c, cols], xt_hi[:, b, c, :], start=(c == 0), stop=False)
                nc.tensor.matmul(dst, wup_lo[:, c, cols], xt_hi[:, b, c, :], start=False, stop=False)
                mm = nc.tensor.matmul(dst, wup_hi[:, c, cols], xt_lo[:, b, c, :], start=False, stop=(c == C - 1))
            mm.then_inc(up_mm, 1)

        def pe_pick(pe, run, k):
            n = run * STEPS + k
            b, e = k // E, k % E
            if e == 0:
                pe.wait_ge(score_t_rdy, run * B + b + 1)
            if n == 0:
                pe.wait_ge(pick_rdy, 1)
            if n == 1:
                pe.wait_ge(elu1_rdy, 2)
            if n >= 2:
                pe.wait_ge(hid_rdy, n - 1)
            nc.tensor.matmul(bank[:, PICK[n % 2], 0:N], pick[:, e, :], score_t[:, b, :], start=True, stop=True).then_inc(pick_mm, 1)

        def pe_down(pe, run, k):
            n = run * STEPS + k
            b, e = k // E, k % E
            nb = run * B + b
            if n == 0:
                pe.wait_ge(bdown_lo_rdy, 1)
            if n < E and n % EQ == 0:
                pe.wait_ge(wdown_lo_rdy, n // EQ + 1)
            if e == 0 and nb < 2:
                pe.wait_ge(elu1_rdy, 3 + nb)
            if e == 0 and nb >= 2:
                pe.wait_ge(out_rdy, (nb - 1) * C)
            pe.wait_ge(hid_hi_rdy, n + 1)
            pe.wait_ge(hid_lo_rdy, n + 1)
            for t in range(C):
                dst = bank[:, DOWN[b % 2], t * D:(t + 1) * D]
                part = slice(t * P, (t + 1) * P)
                if e == 0:
                    nc.tensor.matmul(dst, score_t[:, b, part], bdown_hi[:], start=(t == 0), stop=False, skip_group_check=True)
                    nc.tensor.matmul(dst, score_t[:, b, part], bdown_lo[:], start=False, stop=False, skip_group_check=True)
                nc.tensor.matmul(dst, hid_hi[:, n % HID_SLOTS, part], wdown_hi[:, e, :], start=False, stop=False, skip_group_check=True)
                nc.tensor.matmul(dst, hid_hi[:, n % HID_SLOTS, part], wdown_lo[:, e, :], start=False, stop=False, skip_group_check=True)
                mm = nc.tensor.matmul(dst, hid_lo[:, n % HID_SLOTS, part], wdown_hi[:, e, :], start=False,
                                      stop=(e == E - 1), skip_group_check=True)
            mm.then_inc(down_mm, 1)

        def pe_experts(pe, run):
            for i in range(STEPS + DOWN_LAG):
                b, e = i // E, i % E
                if i < STEPS:
                    pe_up(pe, run, i)
                if PICK_LAG <= i < STEPS + PICK_LAG:
                    pe_pick(pe, run, i - PICK_LAG)
                if e == 0 and 1 <= b < B:
                    pe_gate(pe, run, b)
                if i >= DOWN_LAG:
                    pe_down(pe, run, i - DOWN_LAG)
                if e == 4 and b + 1 < B:
                    pe_xt(pe, run, b + 1)
                if b < B and e == SCORE_PLACE[b]:
                    pe_score(pe, run, b)

        @block.tensor
        def _(pe):
            def turn(b):
                if b == 0:
                    pe.wait_ge(ident_bf_rdy, 1)
                if b >= 2:
                    pe.wait_ge(onehot_t_rdy, b - 1)
                if b == 2:
                    pe.wait_ge(onehot2_rdy, C)
                else:
                    pe.wait_ge(onehot_rdy, C * (b + 1 - b // 3))
                for i in range(C):
                    for j in range(C):
                        mm = nc.tensor.transpose(turned_bank(b)[:, j, i * P:(i + 1) * P],
                                                 onehot[:, C * b + i, j * P:(j + 1) * P], ident_bf[:])
                mm.then_inc(turn_mm, 1)

            def once_part(b):
                if b == 0:
                    pe.wait_ge(ctx_lo_rdy, 1)
                else:
                    pe.wait_ge(once_rdy, b)
                if b < 2:
                    pe.wait_ge(onehot_t_rdy, b + 1)
                else:
                    pe.wait_ge(onehot_t2_rdy, b - 1)
                for i in range(C):
                    for j in range(C):
                        mm = nc.tensor.matmul(bank[:, ONCE, i * P:(i + 1) * P], onehot_t[:, b, j, i * P:(i + 1) * P],
                                              ctx_parts[:, C * b + j, :], start=(j == 0), stop=(j == C - 1))
                mm.then_inc(once_mm, 1)

            def twice_part(b):
                if b >= 1:
                    pe.wait_ge(twice_rdy, b)
                pe.wait_ge(once_rdy, b + 1)
                for j in range(C):
                    mm = nc.tensor.matmul(bank[:, TWICE, 0:N], once[:, b, j, :], onehot_t[:, b, j, :],
                                          start=(j == 0), stop=(j == C - 1))
                mm.then_inc(twice_mm, 1)

            def feat0(b):
                if b == 0:
                    pe.wait_ge(w0_lo_rdy, 1)
                    pe.wait_ge(bias_rdy, 1)
                if b >= 2:
                    pe.wait_ge(h1_rdy, b - 1)
                pe.wait_ge(twice_rdy, b + 1)
                for c in range(C):
                    dst = bank[:, FEAT0[b], c * N:(c + 1) * N]
                    nc.tensor.matmul(dst, bias_parts[:, 0, c * P:(c + 1) * P], ones_r[:], start=True, stop=False)
                    nc.tensor.matmul(dst, w0_hi[:, c * P:(c + 1) * P], twice[:, b, :], start=False, stop=False)
                    mm = nc.tensor.matmul(dst, w0_lo[:, c * P:(c + 1) * P], twice[:, b, :], start=False, stop=True)
                mm.then_inc(feat0_mm, 1)

            def feat1(b):
                if b == 0:
                    pe.wait_ge(w1_lo_rdy, 1)
                pe.wait_ge(h1_lo_rdy, b + 1)
                for t in range(C):
                    dst = bank[:, FEAT1[b], t * D:(t + 1) * D]
                    nc.tensor.matmul(dst, ones_r[:, 0:P], bias_parts[:, 1, :], start=True, stop=False)
                    for c in range(C):
                        rows = slice(t * P, (t + 1) * P)
                        nc.tensor.matmul(dst, h1_hi[:, b, c, rows], w1_hi[:, c, :], start=False, stop=False)
                        nc.tensor.matmul(dst, h1_hi[:, b, c, rows], w1_lo[:, c, :], start=False, stop=False)
                        mm = nc.tensor.matmul(dst, h1_lo[:, b, c, rows], w1_hi[:, c, :], start=False, stop=(c == C - 1))
                mm.then_inc(feat1_mm, 1)

            turn(0)
            once_part(0)
            turn(1)
            twice_part(0)
            once_part(1)
            feat0(0)
            turn(2)
            twice_part(1)
            turn(3)
            once_part(2)
            feat0(1)
            twice_part(2)
            feat1(0)
            once_part(3)
            feat0(2)
            twice_part(3)
            feat0(3)
            feat1(1)
            feat1(2)
            pe_xt(pe, 0, 0)
            feat1(3)
            pe_gate(pe, 0, 0)

            pe_experts(pe, 0)

            def general():
                with pe.Fori(0, B) as b:
                    for l in range(2):
                        if l == 0:
                            pe.wait_ge(g_graph_ld, b * 16 + 16)
                        else:
                            pe.wait_ge(g_h_t, b + 1)
                        for j in range(C):
                            dst = bank[:, 0, j * D:(j + 1) * D]
                            if l == 0:
                                mm = nc.tensor.matmul(dst, ctxt_b[:, j * P:(j + 1) * P], w0_sb[0:FIN, :], start=True, stop=True)
                            else:
                                for c in range(C):
                                    mm = nc.tensor.matmul(dst, gh_t[:, c, j * P:(j + 1) * P], w1_sb[:, c, :],
                                                          start=(c == 0), stop=(c == C - 1))
                        mm.then_inc(g_feat_mm, 1)
                        with pe.Fori(0, H) as h:
                            turn = b * (2 * H) + h + (l * H + 1)
                            pe.wait_ge(g_diag, turn)
                            for j in range(C):
                                mm = nc.tensor.matmul(bank[:, 1, j * P:(j + 1) * P], ones[:], diag[:, j, :],
                                                      start=True, stop=True)
                            mm.then_inc(g_row_mm, 1)
                            pe.wait_ge(g_alpha, turn * 2)
                            for i in range(C):
                                for j in range(C):
                                    mm = nc.tensor.transpose(bank[:, 2, j * N + i * P:j * N + (i + 1) * P],
                                                             alpha[:, i, j * P:(j + 1) * P], ident[:])
                            mm.then_inc(g_alpha_mm, 1)
                            pe.wait_ge(g_alpha_t, turn)
                            for i in range(C):
                                for j in range(C):
                                    mm = nc.tensor.matmul(bank[:, 3, bass.ds(h * FO + i * D, FO)],
                                                          alpha_t[:, j, i * P:(i + 1) * P],
                                                          feat[:, j, bass.ds(h * FO, FO)],
                                                          start=(j == 0), stop=(j == C - 1))
                            mm.then_inc(g_out_mm, 1)
                        if l == 0:
                            pe.wait_ge(g_h, b * 2 + 1)
                            for i in range(C):
                                for c in range(C):
                                    mm = nc.tensor.transpose(bank[:, 4, c * N + i * P:c * N + (i + 1) * P],
                                                             gh[:, i, c * P:(c + 1) * P], ident[:])
                            mm.then_inc(g_h_mm, 1)

                pe_xt(pe, 1, 0)
                pe_gate(pe, 1, 0)
                pe_experts(pe, 1)

            on_general(pe, general)

        def dve_stats(dve, run, b):
            for t in range(C * b, C * b + C):
                nc.vector.bn_stats(stat[:, t, :], xa[:, t, :]).then_inc(stat_rdy, 1)
            for t in range(C * b, C * b + C):
                dve.wait_ge(stat_rdy, NT * run + t + 1)
                nc.vector.bn_aggr(mv[:, t, :], stat[:, t, :]).then_inc(mv_rdy, 1)

        def dve_norm(dve, run, b):
            dve.wait_ge(rstd_rdy, run * B + b + 1)
            for t in range(C * b, C * b + C):
                nc.vector.tensor_scalar(xn[:, t, :], xa[:, t, :], mv[:, t, 0:1], rstd[:, t:t + 1],
                                        ALU.subtract, ALU.mult).then_inc(xn_rdy, 1)

        def dve_xt(dve, run, b):
            dve.wait_ge(xt_hi_rdy, run * B + b + 1)
            nc.vector.tensor_tensor(xt_lo[:, b, :, :], both(XT), xt_hi[:, b, :, :].bitcast(F32), ALU.subtract).then_inc(xt_lo_rdy, 1)

        def dve_gate_sum(dve, run, b):
            dve.wait_ge(gate_mm, run * B + b + 1)
            nc.vector.tensor_reduce(gate_in[:, pair(b), :],
                                    bank[:, ROUTE, 0:C * 2 * E].rearrange("p (t k e) -> p t e k", t=C, k=2),
                                    AX.X, ALU.add).then_inc(gate_in_rdy, 1)

        def dve_logits(dve, run, b):
            nb = run * B + b
            r = pair(b)
            done = [nb * LOGIT_STEPS]

            def link(ins, chained=True):
                done[0] += 1
                ins.then_inc(logit_step, 1)
                if chained:
                    dve.wait_ge(logit_step, done[0])

            dve.wait_ge(gate_h_rdy, nb + 1)
            link(nc.vector.tensor_tensor(gate_prod[:],
                                         gate_h[:, r, :].rearrange("p t (a k) -> p t a k", a=1).broadcast_to([P, C, E, E]),
                                         wg2_sb.rearrange("p (a e) k -> p a e k", a=1).broadcast_to([P, C, E, E]), ALU.mult))
            link(nc.vector.tensor_reduce(logits[:, r, :], gate_prod[:], AX.X, ALU.add))
            for t in range(C * b, C * b + C):
                link(nc.vector.max(ltop[:, t, :], logits[:, t, :]), t == C * b + C - 1)
            nc.vector.tensor_tensor(ldiff[:, r], ltop[:, r, 0], ltop[:, r, 1], ALU.subtract).then_inc(ldiff_rdy, 1)
            for t in range(C * b, C * b + C):
                nc.vector.max_index(lidx[:, t, :], ltop[:, t, :], logits[:, t, :]).then_inc(lidx_rdy, 1)
            assert done[0] == (nb + 1) * LOGIT_STEPS

        def dve_scores(dve, run, b):
            dve.wait_ge(score_mm, run * B + b + 1)
            nc.vector.tensor_copy(score_t[:, b, :], bank[0:2 * E, ROUTE, 0:N]).then_inc(score_t_rdy, 1)

        def dve_weigh(dve, run, k):
            n = run * STEPS + k
            dve.wait_ge(silu_rdy, n + 1)
            dve.wait_ge(pick_mm, n + 1)
            if n >= 2:
                dve.wait_ge(hid_hi_rdy, n - 1)
                dve.wait_ge(hid_lo_rdy, n - 1)
            nc.vector.tensor_tensor(hid[:, n % 2, :], act_out(n), bank[:, PICK[n % 2], 0:N],
                                    ALU.mult).then_inc(hid_rdy, 1)

        def dve_weigh_lo(dve, run, k):
            n = run * STEPS + k
            dve.wait_ge(hid_hi_rdy, n + 1)
            if n >= HID_SLOTS:
                dve.wait_ge(down_mm, n - HID_SLOTS + 1)
            nc.vector.tensor_tensor(hid_lo[:, n % HID_SLOTS, :], hid[:, n % 2, :], hid_hi[:, n % HID_SLOTS, :].bitcast(F32),
                                    ALU.subtract).then_inc(hid_lo_rdy, 1)

        def dve_finish(dve, run, b):
            if run == 1 and b == 0:
                dve.wait_ge(stored, 16 * (B - 1 + C))
            dve.wait_ge(down_mm, (run * B + b + 1) * E)
            for t in range(C):
                nc.vector.scalar_tensor_tensor(out=out_sb[:, C * b + t, :], in0=bank[:, DOWN[b % 2], t * D:(t + 1) * D],
                                               scalar=gates[:, 1:2], in1=xa[:, C * b + t, :],
                                               op0=ALU.mult, op1=ALU.add).then_inc(out_rdy, 1)

        def dve_experts(dve, run, extra):
            for i in range(STEPS + PICK_LAG + 1):
                b, e = i // E, i % E
                if PICK_LAG <= i < STEPS + PICK_LAG:
                    dve_weigh(dve, run, i - PICK_LAG)
                if i > PICK_LAG:
                    dve_weigh_lo(dve, run, i - PICK_LAG - 1)
                if e == 1 and 1 <= b < B:
                    dve_gate_sum(dve, run, b)
                if e == 2 and 1 <= b < B:
                    dve_logits(dve, run, b)
                for step in extra.get(i, ()):
                    step()
                if e == 4 and b >= 2:
                    dve_finish(dve, run, b - 2)
                if b + 1 < B and e == (5 if b else 1):
                    dve_xt(dve, run, b + 1)
                if b < B and e == SCORE_PLACE[b]:
                    dve_scores(dve, run, b)
                if e == 7 and b + 2 < B:
                    dve_norm(dve, run, b + 2)
            dve_finish(dve, run, B - 1)

        @block.vector
        def _(dve):
            nc.vector.memset(ones_r[:].bitcast(F32), 1.0).then_inc(ones_r_rdy, 1)
            nc.vector.memset(bias_sb[:], 0.0).then_inc(bias_zero, 1)
            nc.vector.memset(peaks[:], 0.0).then_inc(peaks_part, 1)

            def rows_top(b):
                dve.wait_ge(x_in[b], 16)
                for t in range(C * b, C * b + C):
                    nc.vector.max(top[:, t, :], x_sb[:, t, :]).then_inc(top_rdy, 1)

            def rows_onehot(b):
                for t in range(C * b, C * b + C):
                    dve.wait_ge(top_rdy, t + 1)
                    nc.vector.tensor_scalar(onehot[:, t, :], x_sb[:, t, :], top[:, t, 0:1], None,
                                            ALU.is_equal).then_inc(onehot_rdy, 1)

            def turned(b):
                dve.wait_ge(turn_mm, b + 1)
                nc.vector.tensor_copy(onehot_t[:, b, :, :], turned_bank(b)).then_inc(onehot_t2_rdy, 1)

            def elu0(b):
                dve.wait_ge(exp0_rdy, b + 1)
                nc.vector.scalar_tensor_tensor(out=h1[:, b, :, :], in0=elu_exp[:, b, :, :], scalar=-1.0,
                                               in1=both(FEAT0[b]), op0=ALU.add, op1=ALU.max).then_inc(h1_rdy, 1)

            def elu0_hi(b):
                dve.wait_ge(h1_rdy, b + 1)
                nc.vector.tensor_copy(h1_hi[:, b, :, :], h1[:, b, :, :]).then_inc(h1_hi_rdy, 1)

            def elu0_lo(b):
                if b < 2:
                    dve.wait_ge(h1_hi_rdy, b + 1)
                else:
                    dve.wait_ge(h1_hi2_rdy, b - 1)
                nc.vector.tensor_tensor(h1_lo[:, b, :, :], h1[:, b, :, :], h1_hi[:, b, :, :].bitcast(F32),
                                        ALU.subtract).then_inc(h1_lo_rdy, 1)

            def elu1(b):
                dve.wait_ge(exp1_rdy, b + 1)
                nc.vector.scalar_tensor_tensor(out=elu_exp[:, b, :, :], in0=elu_exp[:, b, :, :], scalar=-1.0,
                                               in1=both(FEAT1[b]), op0=ALU.add, op1=ALU.max).then_inc(elu1_rdy, 1)

            def gated(b):
                dve.wait_ge(elu1_rdy, b + 1)
                if b == 0:
                    dve.wait_ge(gates_rdy, 1)
                nc.vector.scalar_tensor_tensor(out=xa[:, pair(b), :], in0=elu_exp[:, b, :, :], scalar=gates[:, 0:1],
                                               in1=x_sb[:, pair(b), :], op0=ALU.mult, op1=ALU.add).then_inc(xa_rdy, 1)

            def stats(b):
                dve.wait_ge(xa_rdy, b + 1)
                dve_stats(dve, 0, b)

            rows_top(0)
            rows_onehot(0)
            dve.wait_ge(ctx_hi_rdy, 1)
            nc.vector.tensor_tensor(ctx_parts[:, :, FIN:2 * FIN], ctx_sb[:], ctx_parts[:, :, 0:FIN].bitcast(F32),
                                    ALU.subtract).then_inc(ctx_lo_rdy, 1)
            rows_top(1)
            rows_onehot(1)
            dve.wait_ge(small_ld, 16)
            nc.vector.tensor_copy(wg1_parts[:, :, 0:E], wg1_sb).then_inc(wg1_hi_rdy, 1)
            dve.wait_ge(wg1_hi_rdy, 1)
            nc.vector.tensor_tensor(wg1_parts[:, :, E:2 * E], wg1_sb, wg1_parts[:, :, 0:E].bitcast(F32),
                                    ALU.subtract).then_inc(wg1_lo_rdy, 1)
            dve.wait_ge(w0_hi_rdy, 1)
            nc.vector.tensor_tensor(w0_lo[:], w0_sb, w0_hi[:].bitcast(F32), ALU.subtract).then_inc(w0_lo_rdy, 1)
            rows_top(2)
            dve.wait_ge(bias_hi_rdy, 1)
            nc.vector.tensor_tensor(bias_parts[32:33, :, :], bias_sb[32:33, :, :], bias_parts[32:33, :, :].bitcast(F32),
                                    ALU.subtract).then_inc(bias_rdy, 1)
            rows_top(3)
            rows_onehot(3)
            dve.wait_ge(w1_ld, 16)
            nc.vector.tensor_copy(w1_hi[:], w1_sb[:]).then_inc(w1_hi_rdy, 1)
            dve.wait_ge(wup_ld, 16)
            nc.vector.tensor_copy(wup_hi[:, :, quarter(0)[0]], wup_sb[:, :, quarter(0)[0]]).then_inc(wup_hi_rdy, 1)
            turned(2)
            elu0(0)
            elu0_hi(0)
            elu0_lo(0)
            dve.wait_ge(bdown_ld, 16)
            nc.vector.tensor_copy(bdown_hi[:], bdown_sb[:]).then_inc(bdown_hi_rdy, 1)
            turned(3)
            elu0(1)
            elu0_hi(1)
            elu0_lo(1)
            elu1(0)
            gated(0)
            elu0(2)
            stats(0)
            elu0_lo(2)
            elu0(3)
            dve_norm(dve, 0, 0)
            elu0_lo(3)
            elu1(1)
            dve_xt(dve, 0, 0)
            elu1(2)
            gated(1)
            dve_gate_sum(dve, 0, 0)
            stats(1)
            dve_logits(dve, 0, 0)
            elu1(3)
            gated(2)
            dve_norm(dve, 0, 1)

            def bdown_part():
                dve.wait_ge(bdown_hi_rdy, 1)
                nc.vector.tensor_tensor(bdown_lo[:], bdown_sb[:], bdown_hi[:].bitcast(F32), ALU.subtract).then_inc(bdown_lo_rdy, 1)

            def wdown_part(q):
                _, es = quarter(q)
                dve.wait_ge(wdown_ld, 16)
                nc.vector.tensor_copy(wdown_hi[:, es, :], wdown_sb[:, es, :]).then_inc(wdown_hi_rdy, 1)

            def pick_copy():
                dve.wait_ge(pick_raw, 2)
                nc.vector.tensor_copy(pick[:], pick_f).then_inc(pick_rdy, 1)

            def check_peaks():
                w0t = check_sb[:, 0:C * FIN].rearrange("p (c k) -> p c k", c=C)
                w1t = check_sb[:, C * FIN:].rearrange("p (c k) -> p c k", c=C)
                dve.wait_ge(check_ld, 32)
                dve.wait_ge(peaks_part, 1)
                nc.vector.tensor_reduce(peaks[:, 0:1], ctx_sb[:], AX.XY, ALU.max, apply_absolute_value=True).then_inc(peaks_part, 1)
                nc.vector.tensor_reduce(colsum[:, 0:2], w0t, AX.X, ALU.add, apply_absolute_value=True).then_inc(peaks_part, 1)
                nc.vector.tensor_reduce(colsum[:, 2:4], w1t, AX.X, ALU.add, apply_absolute_value=True).then_inc(peaks_part, 1)
                nc.vector.tensor_reduce(peaks[0:H, 3:7], a_sb[:], AX.X, ALU.add, apply_absolute_value=True).then_inc(peaks_part, 1)
                nc.vector.tensor_reduce(peaks[:, 7:8], b0_sb, AX.X, ALU.max, apply_absolute_value=True).then_inc(peaks_part, 1)
                dve.wait_ge(peaks_part, 6)
                nc.vector.tensor_reduce(peaks[:, 1:3], colsum[:].rearrange("p (k c) -> p k c", c=2), AX.X, ALU.max
                                        ).then_inc(peaks_rdy, 1)

            def check_flag():
                dve.wait_ge(good_rdy, 1)
                nc.vector.tensor_reduce(flag_f[:], good_all[:], AX.X, ALU.min).then_inc(flag_step, 1)
                dve.wait_ge(flag_step, 1)
                nc.vector.tensor_scalar(flag_f[:], flag_f[:], float(P), None, ALU.is_lt).then_inc(flag_step, 1)
                dve.wait_ge(flag_step, 2)
                nc.vector.tensor_copy(flag[:], flag_f[:]).then_inc(flag_rdy, 1)

            dve_experts(dve, 0, {0: [lambda: gated(3), lambda: wdown_part(0)], 1: [lambda: stats(2)],
                                 2: [pick_copy, lambda: wdown_part(1)], 3: [bdown_part], 8: [lambda: wdown_part(2)],
                                 9: [lambda: wdown_part(3)], 12: [lambda: stats(3)], 13: [check_peaks],
                                 STEPS: [check_flag]})

            def general():
                nc.vector.memset(nmax[:], 0.0).then_inc(g_xa, 1)
                for t in range(NT):
                    nc.vector.bn_stats(xstat[:, t, :], x_sb[:, t, :]).then_inc(g_stat, 1)
                for t in range(NT):
                    dve.wait_ge(g_stat, t + 1)
                    nc.vector.bn_aggr(xmv[:, t, :], xstat[:, t, :]).then_inc(g_mv, 1)
                dve.wait_ge(g_mv, NT)
                with dve.Fori(0, B) as b:
                    def link(ins, base):
                        ins.then_inc(g_vec, 1)
                        dve.wait_ge(g_vec, base)

                    g0 = b * VEC_GRAPH
                    link(nc.vector.tensor_scalar(gve[:], xmv[:, bass.ds(b * C, C), 1], EPS, None, ALU.add), g0 + 1)
                    dve.wait_ge(g_sqrt, b + 1)
                    link(nc.vector.reciprocal(grstd[:], grstd[:]), g0 + 2)
                    for c in range(C):
                        rows = x_sb[:, bass.ds(b * C + c, 1), :].rearrange("p a n -> p (a n)")
                        link(nc.vector.tensor_scalar(mask[:, c, :], rows, xmv[:, bass.ds(b * C + c, 1), 0],
                                                     grstd[:, c:c + 1], ALU.subtract, ALU.mult), g0 + (3 + c))
                    link(nc.vector.tensor_scalar(mask, mask, -1.0, 1.0, ALU.mult, ALU.add), g0 + 5)
                    link(nc.vector.tensor_scalar(mask, mask, -MASK, None, ALU.mult), g0 + 6)
                    dve.wait_ge(g_bc_ld, 96)
                    for l in range(2):
                        l0 = g0 + (6 + l * VEC_LAYER)
                        dve.wait_ge(g_feat, b * 2 + (l + 1))
                        for k in range(2):
                            link(nc.vector.tensor_tensor(fprod, feat,
                                                         a_bc[2 * l + k].broadcast_to([P, C, H * FO]),
                                                         ALU.mult), l0 + (2 * k + 1))
                            nc.vector.tensor_reduce(att[:, k, :, :], fprod.rearrange("p c (h o) -> p c h o", h=H),
                                                    AX.X, ALU.add).then_inc(g_vec, 1)
                            if k == 0:
                                dve.wait_ge(g_vec, l0 + 2)
                        with dve.Fori(0, H) as h:
                            turn = b * (2 * H) + h + (l * H + 1)
                            h0 = l0 + h * VEC_HEAD + 4
                            dve.wait_ge(g_vec, l0 + 4)
                            for j in range(C):
                                ins = nc.vector.tensor_scalar(diag[:, j, :], ident[:], att[:, 1, j, bass.ds(h, 1)], None, ALU.mult)
                            ins.then_inc(g_diag, 1)
                            dve.wait_ge(g_row_mm, turn)
                            for i in range(C):
                                link(nc.vector.tensor_scalar(sc[:, i, :], bank[:, 1, 0:N], att[:, 0, i, bass.ds(h, 1)],
                                                             None, ALU.add), h0 + (1 + i))
                            link(nc.vector.scalar_tensor_tensor(out=sc2, in0=sc, scalar=LRELU, in1=sc,
                                                                op0=ALU.mult, op1=ALU.max), h0 + 3)
                            link(nc.vector.tensor_tensor(sc2, sc2, mask, ALU.add), h0 + 4)
                            nc.vector.tensor_reduce(nmax[:], sc2, AX.X, ALU.max, negate=True).then_inc(g_max, 1)
                            dve.wait_ge(g_exp, turn * 2)
                            link(nc.vector.reciprocal(rsum[:], psum_p[:]), h0 + 5)
                            for i in range(C):
                                nc.vector.tensor_scalar(alpha[:, i, :], pr[:, i, :], rsum[:, i:i + 1], None,
                                                        ALU.mult).then_inc(g_alpha, 1)
                        dve.wait_ge(g_out_mm, b * (2 * H) + (l + 1) * H)
                        nc.vector.tensor_tensor(gz, bank[:, 3, :].rearrange("p (c n) -> p c n", c=C),
                                                b_bc[:, l:l + 1, :].broadcast_to([P, C, H * FO]), ALU.add).then_inc(g_z, 1)
                        dve.wait_ge(g_zexp, b * 2 + (l + 1))
                        nc.vector.scalar_tensor_tensor(out=gh, in0=gexp, scalar=-1.0, in1=gz, op0=ALU.add,
                                                       op1=ALU.max).then_inc(g_h, 1)
                        dve.wait_ge(g_h, b * 2 + (l + 1))
                    nc.vector.scalar_tensor_tensor(out=xa[:, bass.ds(b * C, C), :], in0=gh, scalar=gates[:, 0:1], in1=x_sb[:, bass.ds(b * C, C), :],
                                                   op0=ALU.mult, op1=ALU.add).then_inc(g_xa, 1)
                    dve.wait_ge(g_xa, b + 2)

                for b in range(B):
                    dve_stats(dve, 1, b)
                for b in range(2):
                    dve_norm(dve, 1, b)
                dve_xt(dve, 1, 0)
                dve_gate_sum(dve, 1, 0)
                dve_logits(dve, 1, 0)
                dve_experts(dve, 1, {})

            on_general(dve, general)


_OUT = ("out", (B, N, D))


def kernel(x, ctx_512, g_xattn, g_ffn, L0_xattn_W0, L0_xattn_a_self0, L0_xattn_a_neigh0, L0_xattn_b0, L0_xattn_W1,
           L0_xattn_a_self1, L0_xattn_a_neigh1, L0_xattn_b1, L0_ffn_Wg1, L0_ffn_Wg2, L0_ffn_Wup, L0_ffn_bup,
           L0_ffn_Wdown, L0_ffn_bdown):
    import concourse.bacc as bacc
    from concourse.bass_utils import run_bass_kernel_spmd

    def a(v):
        return np.asarray(v)

    def by_partition(v):
        return v.reshape(-1, P, v.shape[-1]).transpose(1, 0, 2).reshape(P, -1)

    ctx = a(ctx_512).reshape(T, FIN)
    w0 = a(L0_xattn_W0).transpose(1, 0, 2).reshape(FIN, H * FO)
    w1 = a(L0_xattn_W1).transpose(1, 0, 2).reshape(H * FO, H * FO)
    b0 = a(L0_xattn_b0).reshape(1, H * FO)
    b1 = a(L0_xattn_b1).reshape(1, H * FO)
    small = np.concatenate([
        np.concatenate([w0, w0], axis=0),
        b0.reshape(C, P).T,
        np.broadcast_to(np.concatenate([a(g_xattn), a(g_ffn)]).reshape(1, 2), (P, 2)),
        a(L0_ffn_bup).T,
        by_partition(a(L0_ffn_Wg1).T),
        np.broadcast_to(a(L0_ffn_Wg2).reshape(1, E * E), (P, E * E)),
    ], axis=1)
    arrays = {
        "x": a(x),
        "ctx": by_partition(ctx),
        "ctx_t": ctx.T,
        "small": small,
        "w1": by_partition(w1),
        "bias_2": np.stack([np.concatenate([b0, b1], axis=0)] * 2),
        "b0_r": b0,
        "b1_r": b1,
        "wup": by_partition(a(L0_ffn_Wup).reshape(E * HE, D).T),
        "wdown": a(L0_ffn_Wdown).transpose(2, 0, 1).reshape(HE, E * D),
        "bdown_2": np.concatenate([a(L0_ffn_bdown), a(L0_ffn_bdown)], axis=0),
        "check_w": np.concatenate([by_partition(w0.T), by_partition(w1.T)], axis=1),
        "avec": np.stack([a(L0_xattn_a_self0), a(L0_xattn_a_neigh0), a(L0_xattn_a_self1), a(L0_xattn_a_neigh1)]),
    }
    nc = bacc.Bacc("TRN2", target_bir_lowering=False, num_devices=1)
    feed, args = {}, []
    for name, v in arrays.items():
        feed[f"in_{name}"] = np.ascontiguousarray(v)
        args.append(nc.dram_tensor(f"in_{name}", v.shape, mybir.dt.from_np(v.dtype), kind="ExternalInput").ap())
    args.append(nc.dram_tensor(_OUT[0], _OUT[1], F32, kind="ExternalOutput").ap())
    args[8] = args[8].rearrange("p (c n) -> p c n", c=C)
    args[4] = args[4].rearrange("p (c n) -> p c n", c=C)
    args[9] = args[9].rearrange("p (e n) -> p e n", e=E)
    args[1] = args[1].rearrange("p (t k) -> p t k", t=NT)
    build(nc, *args)
    r = run_bass_kernel_spmd(nc, [feed], core_ids=[0])
    return r.results[0][_OUT[0]]
```
